# Optimizing a Trainium2 kernel written in Bass

```python
import numpy as np
import jax
import jax.numpy as jnp

def _softmax(x, axis=-1):
    return jax.nn.softmax(x, axis=axis)

def _gelu(x):
    return jax.nn.gelu(x, approximate=True)

def _silu(x):
    return jax.nn.silu(x)

def _sigmoid(x):
    return jax.nn.sigmoid(x)

def _layernorm(x, axis=-1, eps=1e-05):
    m = jnp.mean(x, axis=axis, keepdims=True)
    v = jnp.var(x, axis=axis, keepdims=True)
    return (x - m) / jnp.sqrt(v + eps)

def _scatter_add(tgt, idx, src, axis=0):
    return tgt.at[idx].add(src)

def _segment_sum(src, seg, n):
    return jax.ops.segment_sum(src, seg, n)
kernel_name = 'mk_macaron_d1_jaxref_r8_235b13'

def setup_inputs(seed: int=0):
    np.random.seed(seed)
    _w = jnp.asarray

    def _L0_attn_setup():
        import jax, jax.numpy as jnp
        import numpy as np
        import math
        N_HEAD = 16
        HEAD_DIM = 64
        N_EMBD = 128
        EPS_RMS = 1e-05
        U_L2_EPS = 1e-06

        def _get_alibi_slopes(n_heads):

            def pow2(n):
                start = 2 ** (-2 ** (-(math.log2(n) - 3)))
                return [start * start ** i for i in range(n)]
            if math.log2(n_heads).is_integer():
                return pow2(n_heads)
            c = 2 ** math.floor(math.log2(n_heads))
            s = pow2(c)
            extra = _get_alibi_slopes(2 * c)
            return s + extra[0::2][:n_heads - c]

        def _rmsnorm(x, w):
            var = jnp.mean(jnp.square(x), axis=-1, keepdims=True)
            return x * jax.lax.rsqrt(var + EPS_RMS) * w
        key = jax.random.key(seed)
        ks = jax.random.split(key, 9)
        B, T = (2, 256)
        H, D, C = (N_HEAD, HEAD_DIM, N_EMBD)
        x = jax.random.normal(ks[0], (B, T, C), dtype=jnp.float32)
        sc = 1.0 / math.sqrt(C)
        Wq = jax.random.normal(ks[1], (C, H * D), dtype=jnp.float32) * sc
        Wk = jax.random.normal(ks[2], (C, H * D), dtype=jnp.float32) * sc
        Wv = jax.random.normal(ks[3], (C, H * D), dtype=jnp.float32) * sc
        Wproj = jax.random.normal(ks[4], (H * D, C), dtype=jnp.float32) * (0.5 / math.sqrt(C) / math.sqrt(12))
        q_rms_w = jnp.ones((D,), dtype=jnp.float32)
        k_rms_w = jnp.ones((D,), dtype=jnp.float32)
        omega = jnp.full((H,), math.log(math.expm1(1.0)), dtype=jnp.float32)
        u = jax.random.normal(ks[5], (H, D), dtype=jnp.float32) * (1.0 / math.sqrt(D))
        return {'x': x, 'Wq': Wq, 'Wk': Wk, 'Wv': Wv, 'Wproj': Wproj, 'q_rms_w': q_rms_w, 'k_rms_w': k_rms_w, 'omega': omega, 'u': u}
    _L0_attn_in = _L0_attn_setup()

    def _L0_ffn_setup():
        import jax, jax.numpy as jnp
        import numpy as np
        LORA_DIM = 16
        LORA_TOKEN_INDEX = 1
        B, S, D, H = (4, 256, 128, 512)
        key = jax.random.key(seed)
        ks = jax.random.split(key, 6)
        x = jax.random.normal(ks[0], (B, S, D), dtype=jnp.float32)
        W1 = jax.random.normal(ks[1], (H, D), dtype=jnp.float32) * 0.02
        b1 = jnp.zeros((H,), dtype=jnp.float32)
        W2 = jax.random.normal(ks[2], (D, H), dtype=jnp.float32) * 0.02
        b2 = jnp.zeros((D,), dtype=jnp.float32)
        scale = jnp.asarray(0.001, dtype=jnp.float32)
        return {'x': x, 'W1': W1, 'b1': b1, 'W2': W2, 'b2': b2, 'scale': scale}
    _L0_ffn_in = _L0_ffn_setup()
    _d = {'L0_attn_x': _L0_attn_in['x'], 'L0_attn_Wq': _L0_attn_in['Wq'], 'L0_attn_Wk': _L0_attn_in['Wk'], 'L0_attn_Wv': _L0_attn_in['Wv'], 'L0_attn_Wproj': _L0_attn_in['Wproj'], 'L0_attn_q_rms_w': _L0_attn_in['q_rms_w'], 'L0_attn_k_rms_w': _L0_attn_in['k_rms_w'], 'L0_attn_omega': _L0_attn_in['omega'], 'L0_attn_u': _L0_attn_in['u'], 'L0_ffn_W1': _L0_ffn_in['W1'], 'L0_ffn_b1': _L0_ffn_in['b1'], 'L0_ffn_W2': _L0_ffn_in['W2'], 'L0_ffn_b2': _L0_ffn_in['b2'], 'L0_ffn_scale': _L0_ffn_in['scale']}
    _x0 = _d['L0_attn_x']
    _d['L0_attn_x'] = jax.random.normal(jax.random.fold_in(jax.random.key(seed), 1), (8, 512, 128), dtype=_x0.dtype)
    del _x0
    return _d

def reference(L0_attn_x, L0_attn_Wq, L0_attn_Wk, L0_attn_Wv, L0_attn_Wproj, L0_attn_q_rms_w, L0_attn_k_rms_w, L0_attn_omega, L0_attn_u, L0_ffn_W1, L0_ffn_b1, L0_ffn_W2, L0_ffn_b2, L0_ffn_scale):

    def _L0_attn_ref(x, Wq, Wk, Wv, Wproj, q_rms_w, k_rms_w, omega, u):
        import jax, jax.numpy as jnp
        import numpy as np
        import math
        N_HEAD = 16
        HEAD_DIM = 64
        N_EMBD = 128
        EPS_RMS = 1e-05
        U_L2_EPS = 1e-06

        def _get_alibi_slopes(n_heads):

            def pow2(n):
                start = 2 ** (-2 ** (-(math.log2(n) - 3)))
                return [start * start ** i for i in range(n)]
            if math.log2(n_heads).is_integer():
                return pow2(n_heads)
            c = 2 ** math.floor(math.log2(n_heads))
            s = pow2(c)
            extra = _get_alibi_slopes(2 * c)
            return s + extra[0::2][:n_heads - c]

        def _rmsnorm(x, w):
            var = jnp.mean(jnp.square(x), axis=-1, keepdims=True)
            return x * jax.lax.rsqrt(var + EPS_RMS) * w
        B, T, C = x.shape
        H, D = (N_HEAD, HEAD_DIM)
        q = (x @ Wq).reshape(B, T, H, D)
        k = (x @ Wk).reshape(B, T, H, D)
        v = (x @ Wv).reshape(B, T, H, D)
        q = _rmsnorm(q, q_rms_w)
        k = _rmsnorm(k, k_rms_w)
        slopes = jnp.asarray(_get_alibi_slopes(H), dtype=jnp.float32)
        omega_eff = jax.nn.softplus(omega) * slopes
        u_n = u / jnp.maximum(jnp.linalg.norm(u, axis=-1, keepdims=True), U_L2_EPS)
        gate_logits = jnp.einsum('bthd,hd->bht', k, u_n) / math.sqrt(D)
        gate = jax.nn.softplus(gate_logits)
        idx = jnp.arange(T)
        dist = jnp.maximum(idx[:, None] - idx[None, :], 0).astype(jnp.float32)
        bias = -dist[None, None] * omega_eff[None, :, None, None] * gate[:, :, None, :]
        causal = idx[:, None] >= idx[None, :]
        bias = jnp.where(causal[None, None], bias, -jnp.inf)
        scale = 1.0 / math.sqrt(D)
        scores = jnp.einsum('bihd,bjhd->bhij', q, k) * scale + bias
        attn = jax.nn.softmax(scores, axis=-1)
        y = jnp.einsum('bhij,bjhd->bihd', attn, v).reshape(B, T, H * D)
        return y @ Wproj

    def _L0_ffn_ref(x, W1, b1, W2, b2, scale):
        import jax, jax.numpy as jnp
        import numpy as np
        LORA_DIM = 16
        LORA_TOKEN_INDEX = 1
        B, S, D, H = (4, 256, 128, 512)
        Bx, Sx, Dx = x.shape
        Hx = W1.shape[0]
        lt = jax.lax.dynamic_slice_in_dim(x, LORA_TOKEN_INDEX, LORA_DIM, axis=1)
        even = lt[:, ::2, :]
        odd = lt[:, 1::2, :]
        m1 = (even[:, :4, :, None] * odd[:, :4, None, :]).reshape(Bx, Hx, Dx)
        m2 = (even[:, 4:, :, None] * odd[:, 4:, None, :]).reshape(Bx, Dx, Hx)
        h = jnp.einsum('bsd,hd->bsh', x, W1) + scale * jnp.einsum('bsd,bhd->bsh', x, m1) + b1
        h = jax.nn.gelu(h, approximate=False)
        out = jnp.einsum('bsh,oh->bso', h, W2) + scale * jnp.einsum('bsh,boh->bso', h, m2) + b2
        return out
    x = L0_attn_x
    x = x + 0.5 * _L0_ffn_ref(_layernorm(x, axis=-1), L0_ffn_W1, L0_ffn_b1, L0_ffn_W2, L0_ffn_b2, L0_ffn_scale)
    x = x + _L0_attn_ref(_layernorm(x, axis=-1), L0_attn_Wq, L0_attn_Wk, L0_attn_Wv, L0_attn_Wproj, L0_attn_q_rms_w, L0_attn_k_rms_w, L0_attn_omega, L0_attn_u)
    x = x + 0.5 * _L0_ffn_ref(_layernorm(x, axis=-1), L0_ffn_W1, L0_ffn_b1, L0_ffn_W2, L0_ffn_b2, L0_ffn_scale)
    return x

_drawn_inputs = setup_inputs


def setup_inputs(seed=0):
    import zlib

    import numpy as np

    out = dict(_drawn_inputs(seed))
    spreads = {'L0_attn_q_rms_w': (1.0, 0.6),
     'L0_attn_k_rms_w': (1.0, 0.6),
     'L0_attn_omega': (0.5413248538970947, 0.6),
     'L0_ffn_b1': (0.0, 0.317),
     'L0_ffn_b2': (0.0, 0.1)}
    factors = {'L0_attn_u': 7.111}
    for name, (base, spread) in spreads.items():
        noise = np.random.default_rng([zlib.crc32(name.encode()), seed]).standard_normal(out[name].shape)
        drawn = base * np.exp(spread * noise) if base else spread * noise
        out[name] = jnp.asarray(drawn.astype(out[name].dtype))
    for name, factor in factors.items():
        out[name] = (out[name] * factor).astype(out[name].dtype)
    return out
```

```python
import math
from contextlib import ExitStack

import concourse.bass as bass
from concourse import mybir

ALU = mybir.AluOpType
ACT = mybir.ActivationFunctionType
AX = mybir.AxisListType
F32 = mybir.dt.float32
F16 = mybir.dt.float16

P = 128
LN_EPS = 1e-5
RMS_EPS = 1e-5
U_EPS = 1e-6
W_UP = 64.0
QKV_UP = 16.0
MASKED = -60000.0


def slopes_of(heads):
    start = 2.0 ** (-2.0 ** (-(math.log2(heads) - 3)))
    return [start * start ** i for i in range(heads)]


def macaron(nc: bass.Bass, x, Wq, Wk, Wv, Wproj, q_rms_w, k_rms_w, omega, u, W1, b1, W2, b2, scale, out):
    B, T, C = x.shape
    H, D = u.shape
    HD = H * D
    F = W1.shape[0]
    TB = T // P
    FB = F // P
    NP = H // 2
    RPT = 128 // FB
    assert C == P and T == 512 and F == 512 and D == 64 and TB == 4 and FB == 4
    REGION = {0: (0, 512), 1: (512, 384), 3: (896, 128), 2: (1024, 256)}
    SCOLS = 1280

    with ExitStack() as ctx:
        def sb(name, shape, dt=F32):
            return ctx.enter_context(nc.sbuf_tensor(name, shape, dt))

        def sem(name):
            return ctx.enter_context(nc.semaphore(name))

        ps = ctx.enter_context(nc.psum_tensor("ps", [P, 8, 512], F32))
        ps_flat = ps[:, :, :].rearrange("p a n -> p (a n)")

        ident = sb("ident", [P, P])
        ident16 = sb("ident16", [P, P], F16)
        causal16 = sb("causal16", [P, P], F16)
        causal_t16 = sb("causal_t16", [P, P], F16)
        ones = sb("ones", [P, D])
        neghalf = sb("neghalf", [P, 32])
        half = sb("half", [P, H])
        sel = sb("sel", [P, 4, P])
        jcol = sb("jcol", [P, TB])
        icol = sb("icol", [P, T])
        icol16 = sb("icol16", [P, T], F16)
        zrow = sb("zrow", [H, T], F16)
        w1s = sb("w1s", [P, F])
        w2s = sb("w2s", [P, F])
        wqkv_h = sb("wqkv_h", [P, 3 * HD], F16)
        wqkv_l = sb("wqkv_l", [P, 3 * HD], F16)
        wp_h = sb("wp_h", [P, NP, C], F16)
        wp_l = sb("wp_l", [P, NP, C], F16)
        wu = sb("wu", [P, H])
        wu_h = sb("wu_h", [P, H], F16)
        wu_l = sb("wu_l", [P, H], F16)
        b1c = sb("b1c", [P, FB])
        b2c = sb("b2c", [P, 1])
        b2half = sb("b2half", [P, 1])
        sc = sb("sc", [P, 1])
        sc_up = sb("sc_up", [P, 1])
        qw = sb("qw", [P, 1])
        kw = sb("kw", [P, 1])
        qws = sb("qws", [P, 1])
        kws = sb("kws", [P, 1])
        om = sb("om", [P, H])
        om_e = sb("om_e", [P, H])
        om_n = sb("om_n", [P, H])
        slopes = sb("slopes", [P, H])
        un = sb("un", [P, H])
        kwb = sb("kwb", [P, D])
        x_in = sb("x_in", [P, TB, C])
        x_1 = sb("x_1", [P, TB, C])
        x_2 = sb("x_2", [P, TB, C])
        x_out = sb("x_out", [P, TB, C])
        stats = sb("stats", [P, TB, 6])
        mv = sb("mv", [P, TB, 2])
        veps = sb("veps", [P, TB])
        rstd = sb("rstd", [P, TB])
        z = sb("z", [P, TB, C])
        zt_h = sb("zt_h", [P, T], F16)
        zt_l = sb("zt_l", [P, T], F16)
        od = sb("od", [P, 2, P])
        ev = sb("ev", [P, 2, F])
        w1e = sb("w1e", [P, F])
        w2e = sb("w2e", [P, F])
        w1_h = sb("w1_h", [P, F], F16)
        w1_l = sb("w1_l", [P, F], F16)
        w2_h = sb("w2_h", [P, F], F16)
        w2_l = sb("w2_l", [P, F], F16)
        hid_h = sb("hid_h", [P, FB, T], F16)
        hid_l = sb("hid_l", [P, FB, T], F16)
        o_sb = sb("o_sb", [P, T])
        sq = sb("sq", [P, 4, 512])
        ss = sb("ss", [P, TB, 32])
        ssv = sb("ssv", [P, TB, 32])
        rs = sb("rs", [P, TB, 32])
        qkn = sb("qkn", [P, 2, TB, HD])
        v = sb("v", [P, TB, HD])
        q1 = sb("q1", [P, H, T], F16)
        k1 = sb("k1", [P, H, T], F16)
        q2 = sb("q2", [P, H, T], F16)
        k2 = sb("k2", [P, H, T], F16)
        lg = sb("lg", [P, TB, H])
        lgn = sb("lgn", [P, TB, H])
        lga = sb("lga", [P, TB, H])
        lge = sb("lge", [P, TB, H])
        lgl = sb("lgl", [P, TB, H])
        sp_ = sb("sp_", [P, TB, H])
        gate = sb("gate", [P, TB, H])
        jgate = sb("jgate", [P, TB, H])
        gt = sb("gt", [P, TB, 8, H], F16)
        gtt = sb("gtt", [4 * H, T], F16)
        negm = sb("negm", [P, TB, H], F16)
        nmt = sb("nmt", [H, T], F16)
        pt = qkn[:, :, :, :].rearrange("p a t n -> p (a t n)")[:, 0:4 * SCOLS].rearrange("p (a b n) -> p a b n", a=2, b=2)
        vst = sb("vst", [P, 2, TB, 2 * D])
        rden = sb("rden", [P, T])
        yf = sb("yf", [P, T])
        y_h = sq[:, :, :].rearrange("p a n -> p (a n)").bitcast(F16).rearrange("p (a n) -> p a n", a=NP)
        y_l = sb("y_l", [P, NP, T], F16)

        wld = qkn[:, :, :, :].rearrange("p a t n -> p (a t n)")[:, 0:3 * HD]
        ub = qkn[:, :, :, :].rearrange("p a t n -> p (a t n)")[:, 3 * HD:4 * HD]
        uq = qkn[:, :, :, :].rearrange("p a t n -> p (a t n)")[:, 4 * HD:5 * HD]
        wup = qkn[:, :, :, :].rearrange("p a t n -> p (a t n)")[:, 5 * HD:8 * HD]
        wpl = v[:, 0, :].rearrange("p (a n) -> p a n", a=NP)
        wpu = v[:, 1, :].rearrange("p (a n) -> p a n", a=NP)
        w1ld = v[:, 2, 0:F].rearrange("p (a n) -> p a n", a=FB)
        w2ld = v[:, 2, F:2 * F]
        hid = qkn[:, 0, 0:2, :].rearrange("p a n -> p (a n)").rearrange("p (r n) -> p r n", n=T)

        s_wload = sem("s_wload")
        s_const = sem("s_const")
        s_unit = sem("s_unit")
        s_icol = sem("s_icol")
        s_w12_ps = sem("s_w12_ps")
        s_setup = sem("s_setup")
        s_usq = sem("s_usq")
        s_unorm = sem("s_unorm")
        s_omn = sem("s_omn")
        s_oml = sem("s_oml")
        dve_step = sem("dve_step")
        s_rows = sem("s_rows")
        s_x = sem("s_x")
        s_out = sem("s_out")
        LN = ["ffn_a", "att", "ffn_b"]
        s_var = {n: sem(f"s_var_{n}") for n in LN}
        s_rstd = {n: sem(f"s_rstd_{n}") for n in LN}
        s_z = {n: sem(f"s_z_{n}") for n in LN}
        s_zt_ps = {n: sem(f"s_zt_ps_{n}") for n in LN}
        s_zt_h = {n: sem(f"s_zt_h_{n}") for n in LN}
        s_zt_l = {n: sem(f"s_zt_l_{n}") for n in LN}
        s_o_ps = {n: sem(f"s_o_ps_{n}") for n in LN}
        s_o_sb = {n: sem(f"s_o_sb_{n}") for n in LN}
        s_ot_ps = {n: sem(f"s_ot_ps_{n}") for n in LN}
        s_x_new = {n: sem(f"s_x_new_{n}") for n in LN}
        FFN = ["ffn_a", "ffn_b"]
        s_sel_ps = {n: sem(f"s_sel_ps_{n}") for n in FFN}
        s_ev = {n: sem(f"s_ev_{n}") for n in FFN}
        s_m_ps = {n: sem(f"s_m_ps_{n}") for n in FFN}
        s_weff = {n: sem(f"s_weff_{n}") for n in FFN}
        s_wsplit = {n: sem(f"s_wsplit_{n}") for n in FFN}
        s_h_ps = {n: sem(f"s_h_ps_{n}") for n in FFN}
        s_hid = {n: sem(f"s_hid_{n}") for n in FFN}
        s_hid_h = {n: sem(f"s_hid_h_{n}") for n in FFN}
        s_hid_l = {n: sem(f"s_hid_l_{n}") for n in FFN}
        s_qkv_ps = sem("s_qkv_ps")
        s_gl_ps = sem("s_gl_ps")
        s_sq = sem("s_sq")
        s_sqsum = sem("s_sqsum")
        s_ssv = sem("s_ssv")
        s_rs = sem("s_rs")
        s_qkn = sem("s_qkn")
        s_v = sem("s_v")
        s_t_ps = sem("s_t_ps")
        s_hi = sem("s_hi")
        s_lo = sem("s_lo")
        s_dup = sem("s_dup")
        s_lg = sem("s_lg")
        s_lga = sem("s_lga")
        s_lge = sem("s_lge")
        s_lgl = sem("s_lgl")
        s_gt = sem("s_gt")
        s_gt_ps = sem("s_gt_ps")
        s_gtt = sem("s_gtt")
        s_grow = sem("s_grow")
        s_a_ps = sem("s_a_ps")
        s_a_free = sem("s_a_free")
        s_nm_ps = sem("s_nm_ps")
        s_nmt = sem("s_nmt")
        s_mrow = sem("s_mrow")
        s_zero = sem("s_zero")
        s_s_ps = sem("s_s_ps")
        s_exp = sem("s_exp")
        s_vst = sem("s_vst")
        s_pv = sem("s_pv")
        s_rden = sem("s_rden")
        s_y = sem("s_y")
        s_y_h = sem("s_y_h")
        s_y_l = sem("s_y_l")

        block = ctx.enter_context(nc.Block())
        NLOADS = 14

        def row_of(a):
            return a.rearrange("(o n) -> o n", o=1)

        @block.sync
        def _(sp):
            for i, w in enumerate((Wq, Wk, Wv)):
                sp.dma_start(wld[:, i * HD:(i + 1) * HD], w).then_inc(s_wload, 16)
            sp.dma_start(wpl, Wproj.rearrange("(a p) n -> p a n", p=P)).then_inc(s_wload, 16)
            sp.dma_start(w1ld, W1.rearrange("(a p) n -> p a n", p=P)).then_inc(s_wload, 16)
            sp.dma_start(w2ld, W2).then_inc(s_wload, 16)
            sp.dma_start(b1c[:, :], b1.rearrange("(a p) -> p a", p=P), allow_slow_non_contiguous=True).then_inc(s_wload, 16)
            sp.dma_start(b2c[:, :], b2.rearrange("(p o) -> p o", o=1)).then_inc(s_wload, 16)
            sp.dma_start(sc[:, :], row_of(scale).broadcast_to([P, 1])).then_inc(s_wload, 16)
            sp.dma_start(om[:, :], row_of(omega).broadcast_to([P, H])).then_inc(s_wload, 16)
            sp.dma_start(kwb[:, :], row_of(k_rms_w).broadcast_to([P, D])).then_inc(s_wload, 16)
            sp.dma_start(ub, row_of(u.rearrange("h d -> (h d)")).broadcast_to([P, HD])).then_inc(s_wload, 16)
            for half_ in range(2):
                sp.dma_start(qw[half_ * D:(half_ + 1) * D, :],
                             q_rms_w.rearrange("(p o) -> p o", o=1)).then_inc(s_unit, 16)
                sp.dma_start(kw[half_ * D:(half_ + 1) * D, :],
                             k_rms_w.rearrange("(p o) -> p o", o=1)).then_inc(s_unit, 16)
            sp.wait_ge(s_icol, 3)
            for h in range(H):
                sp.dma_start(q1[96:98, h, :], icol16[0:2, :]).then_inc(s_rows, 16)
            sp.wait_ge(s_const, 19)
            sp.dma_start(q1[64:65, :, :], zrow[:, :]).then_inc(s_zero, 16)
            with sp.Fori(0, B) as b:
                sp.wait_ge(s_x_new["ffn_a"], b + 1)
                sp.dma_start(x_in[:, :, :], x[b].rearrange("(t p) c -> p t c", p=P)).then_inc(s_x, 16)
                sp.wait_ge(s_hi, (b + 1) * 2 * H)
                sp.dma_start(q2[0:D, :, :], q1[0:D, :, :]).then_inc(s_dup, 16)
                sp.dma_start(k2[D:2 * D, :, :], k1[0:D, :, :]).then_inc(s_dup, 16)
                sp.wait_ge(s_gtt, b + 1)
                for r in range(4):
                    sp.dma_start(k1[96 + r:97 + r, :, :], gtt[r * H:(r + 1) * H, :]).then_inc(s_grow, 16)
                sp.wait_ge(s_nmt, b + 1)
                sp.dma_start(q1[64:65, :, :], nmt[:, :]).then_inc(s_mrow, 16)
                sp.wait_ge(s_pv, 2 + (b + 1) * NP)
                sp.dma_start(q1[64:65, :, :], zrow[:, :]).then_inc(s_zero, 16)
                sp.wait_ge(s_x_new["ffn_b"], b + 1)
                sp.dma_start(out[b].rearrange("(t p) c -> p t c", p=P), x_out[:, :, :]).then_inc(s_out, 16)
            sp.wait_ge(s_out, 16 * (B + 1))
            sp.wait_ge(s_zero, 16 * (B + 1))

        @block.gpsimd
        def _(pool):
            g = nc.gpsimd
            g.memset(ident[:, :], 0.0).then_inc(s_const, 1)
            g.memset(ident16[:, :], 0.0).then_inc(s_const, 1)
            g.memset(causal16[:, :], 0.0).then_inc(s_const, 1)
            g.memset(causal_t16[:, :], 0.0).then_inc(s_const, 1)
            g.memset(sel[:, :, :], 0.0).then_inc(s_const, 1)
            g.iota(jcol[:, :], [[P, TB]], base=-(T // 2), channel_multiplier=1,
                   allow_small_or_imprecise_dtypes=True).then_inc(s_const, 1)
            g.iota(icol[:, :], [[-1, T]], base=T // 2, channel_multiplier=0,
                   allow_small_or_imprecise_dtypes=True).then_inc(s_icol, 1)
            for t, n in ((ones, 1.0), (neghalf, -0.5), (half, 0.5)):
                g.memset(t[:, :], n).then_inc(s_const, 1)
            g.memset(zrow[:, :], 0.0).then_inc(s_const, 1)
            for h, s in enumerate(slopes_of(H)):
                last = g.memset(slopes[:, h:h + 1], s)
            last.then_inc(s_const, 1)
            pool.wait_ge(s_const, 5)
            for m in (ident, ident16):
                g.affine_select(out=m[:, :], in_=m[:, :], compare_op=ALU.not_equal, fill=1.0, base=0,
                                pattern=[[-1, P]], channel_multiplier=1).then_inc(s_const, 1)
            g.affine_select(out=causal16[:, :], in_=causal16[:, :], compare_op=ALU.is_ge, fill=MASKED, base=0,
                            pattern=[[-1, P]], channel_multiplier=1).then_inc(s_const, 1)
            g.affine_select(out=causal_t16[:, :], in_=causal_t16[:, :], compare_op=ALU.is_ge, fill=MASKED, base=0,
                            pattern=[[1, P]], channel_multiplier=-1).then_inc(s_const, 1)
            for n, first in enumerate((2, 10, 1, 9)):
                s = sel[:, n, :].rearrange("p (r e) -> p r e", r=FB)
                g.affine_select(out=s, in_=s, compare_op=ALU.not_equal, fill=1.0, base=-first,
                                pattern=[[-2, FB], [1000, RPT]], channel_multiplier=1).then_inc(s_const, 1)
            pool.wait_ge(s_const, 19)
            pool.wait_ge(s_usq, 1)
            g.tensor_tensor(un[:, :], om_n[:, :], half[:, :], ALU.pow).then_inc(s_unorm, 1)
            with pool.Fori(0, B) as b:
                def inverse_root(name):
                    pool.wait_ge(s_var[name], b + 1)
                    g.tensor_tensor(rstd[:, :], veps[:, :], neghalf[:, 0:TB], ALU.pow).then_inc(s_rstd[name], 1)

                inverse_root("ffn_a")
                inverse_root("att")
                for t in range(TB):
                    pool.wait_ge(s_ssv, b * TB + t + 1)
                    g.tensor_tensor(rs[:, t, :], ssv[:, t, :], neghalf[:, :], ALU.pow).then_inc(s_rs, 1)
                with pool.Fori(0, NP // 2) as it:
                    pool.wait_ge(s_v, (b + 1) * 2 * TB)
                    for par in range(2):
                        n = b * NP + it * 2 + par
                        pool.wait_ge(s_pv, n + 1)
                        g.tensor_copy(vst[:, par, :, :],
                                      v[:, :, bass.ds((it * 2 + par) * 2 * D, 2 * D)]).then_inc(s_vst, 1)
                inverse_root("ffn_b")

        @block.scalar
        def _(act):
            a = nc.scalar
            act.wait_ge(s_omn, 1)
            a.activation(om_e[:, :], om_n[:, :], ACT.Exp).then_inc(s_oml, 1)
            act.wait_ge(s_oml, 1)
            a.activation(om_n[:, :], om_e[:, :], ACT.Ln, bias=1.0).then_inc(s_oml, 1)

            with act.Fori(0, B) as b:
                def split_z(name):
                    act.wait_ge(s_zt_ps[name], b + 1)
                    a.activation(zt_h[:, :], ps[:, 0, :], ACT.Copy).then_inc(s_zt_h[name], 1)

                def ffn(name):
                    split_z(name)
                    for r in range(FB):
                        act.wait_ge(s_h_ps[name], b * FB + r + 1)
                        a.activation(hid[:, r, :], ps[:, 4 + r, :], ACT.Gelu, bias=b1c[:, r:r + 1],
                                     scale=1.0 / W_UP).then_inc(s_hid[name], 1)
                    act.wait_ge(s_o_ps[name], b + 1)
                    a.activation(o_sb[:, :], ps[:, 0, :], ACT.Identity, bias=b2half[:, :],
                                 scale=0.5 / W_UP).then_inc(s_o_sb[name], 1)

                def attention():
                    split_z("att")
                    for t in range(TB):
                        for c in range(6):
                            act.wait_ge(s_qkv_ps, (b * TB + t) * 6 + c + 1)
                            if c < 4:
                                act.wait_ge(s_sqsum, (b * TB + t) * 4 + 4)
                                a.activation(sq[:, c, :], ps[:, 1 + c, :], ACT.Square).then_inc(s_sq, 1)
                            else:
                                a.activation(v[:, t, (c - 4) * 512:(c - 3) * 512], ps[:, 1 + c, :],
                                             ACT.Copy).then_inc(s_v, 1)
                    act.wait_ge(s_lga, b + 1)
                    a.activation(lge[:, :, :], lga[:, :, :], ACT.Exp).then_inc(s_lge, 1)
                    act.wait_ge(s_lge, b + 1)
                    a.activation(lgl[:, :, :], lge[:, :, :], ACT.Ln, bias=1.0).then_inc(s_lgl, 1)
                    for n in range(2 * NP):
                        act.wait_ge(s_t_ps, b * 2 * NP + n + 1)
                        for hh in range(2):
                            r = slice(hh * D, (hh + 1) * D)
                            dst, w = ((q1, qws), (k1, kws))[n % 2]
                            a.activation(dst[0:D, 2 * (n // 2) + hh, :], ps[r, 1 + n % 4, :], ACT.Identity,
                                         scale=w[r, :]).then_inc(s_hi, 1)
                    with act.Fori(0, NP // 2) as it:
                        for par in range(2):
                            n = b * NP + it * 2 + par
                            act.wait_ge(s_pv, n + 1)
                            for hh in range(2):
                                act.wait_ge(s_s_ps, n * 2 + hh + 1)
                                a.activation(pt[:, par, hh, :], ps_flat[:, hh * 1536:hh * 1536 + SCOLS],
                                             ACT.Exp).then_inc(s_exp, 1)
                    act.wait_ge(s_o_ps["att"], b + 1)
                    a.activation(o_sb[:, :], ps[:, 0, :], ACT.Identity,
                                 scale=1.0 / (W_UP * QKV_UP)).then_inc(s_o_sb["att"], 1)

                ffn("ffn_a")
                attention()
                ffn("ffn_b")

        @block.tensor
        def _(pe):
            pe.wait_ge(s_const, 19)
            pe.wait_ge(s_wload, 16 * 12)
            for r in range(FB):
                pe.transpose(ps[:, 0, r * P:(r + 1) * P], w1ld[:, r, :], ident[:, :]).then_inc(s_w12_ps, 1)
            for r in range(FB):
                pe.transpose(ps[:, 1, r * P:(r + 1) * P], w2ld[:, r * P:(r + 1) * P], ident[:, :]).then_inc(s_w12_ps, 1)
            pe.wait_ge(s_setup, 1)
            pe.wait_ge(s_rows, 16 * H)

            with pe.Fori(0, B) as b:
                def product(dst, ah, al, bh, bl, first=True, last=True):
                    pe.matmul(dst, ah, bh, start=first, stop=False)
                    pe.matmul(dst, ah, bl, start=False, stop=False)
                    return pe.matmul(dst, al, bh, start=False, stop=last)

                def turn(name):
                    pe.wait_ge(s_z[name], (b + 1) * TB)
                    for t in range(TB):
                        mm = pe.transpose(ps[:, 0, t * P:(t + 1) * P], z[:, t, :], ident[:, :])
                    mm.then_inc(s_zt_ps[name], 1)

                def turn_back(name):
                    pe.wait_ge(s_o_sb[name], b + 1)
                    for t in range(TB):
                        mm = pe.transpose(ps[:, 1, t * P:(t + 1) * P], o_sb[:, t * P:(t + 1) * P], ident[:, :])
                    mm.then_inc(s_ot_ps[name], 1)

                def ffn(name):
                    turn(name)
                    for n in range(4):
                        mm = pe.matmul(ps[:, 1, n * P:(n + 1) * P], sel[:, n, :], z[:, 0, :], start=True, stop=True)
                    mm.then_inc(s_sel_ps[name], 1)
                    pe.wait_ge(s_ev[name], b + 1)
                    for n in range(2):
                        mm = pe.matmul(ps[:, 2 + n, :], od[:, n, :], ev[:, n, :], start=True, stop=True)
                    mm.then_inc(s_m_ps[name], 1)
                    pe.wait_ge(s_wsplit[name], b + 1)
                    pe.wait_ge(s_zt_l[name], b + 1)
                    for r in range(FB):
                        c = slice(r * P, (r + 1) * P)
                        product(ps[:, 4 + r, :], w1_h[:, c], w1_l[:, c], zt_h[:, :],
                                zt_l[:, :]).then_inc(s_h_ps[name], 1)
                    for r in range(FB):
                        pe.wait_ge(s_hid_l[name], b * FB + r + 1)
                        c = slice(r * P, (r + 1) * P)
                        mm = product(ps[:, 0, :], w2_h[:, c], w2_l[:, c], hid_h[:, r, :], hid_l[:, r, :],
                                     r == 0, r == FB - 1)
                    mm.then_inc(s_o_ps[name], 1)
                    turn_back(name)

                def attention():
                    turn("att")
                    pe.wait_ge(s_zt_l["att"], b + 1)
                    for t in range(TB):
                        c = slice(t * P, (t + 1) * P)
                        product(ps[:, 7, t * H:(t + 1) * H], zt_h[:, c], zt_l[:, c], wu_h[:, :],
                                wu_l[:, :]).then_inc(s_gl_ps, 1)
                        for n in range(6):
                            if t:
                                if n < 4:
                                    pe.wait_ge(s_qkn, (b * TB + t - 1) * 4 + n + 1)
                                else:
                                    pe.wait_ge(s_v, (b * TB + t - 1) * 2 + n - 3)
                            w = slice(n * 512, (n + 1) * 512)
                            product(ps[:, 1 + n, :], zt_h[:, c], zt_l[:, c], wqkv_h[:, w],
                                    wqkv_l[:, w]).then_inc(s_qkv_ps, 1)
                    pe.wait_ge(s_gt, b + 1)
                    pe.wait_ge(s_v, (b + 1) * 2 * TB)
                    for t in range(TB):
                        mm = pe.transpose(ps[:, 5, :].bitcast(F16)[:, t * P:(t + 1) * P],
                                          gt[:, t, :, :].rearrange("p r h -> p (r h)"), ident16[:, :])
                    mm.then_inc(s_gt_ps, 1)
                    pe.wait_ge(s_qkn, (b + 1) * TB * 4)
                    for n in range(2 * NP):
                        if n >= 4:
                            pe.wait_ge(s_lo, b * 2 * H + 2 * (n - 3))
                        for t in range(TB):
                            mm = pe.transpose(ps[:, 1 + n % 4, t * P:(t + 1) * P],
                                              qkn[:, n % 2, t, (n // 2) * P:(n // 2 + 1) * P], ident[:, :])
                        mm.then_inc(s_t_ps, 1)
                    with pe.Fori(0, H // 2) as it:
                        pe.wait_ge(s_lo, (b + 1) * 2 * H)
                        pe.wait_ge(s_grow, 64 * (b + 1))
                        pe.wait_ge(s_zero, 16 * (b + 1))
                        for par in range(2):
                            h = it * 2 + par
                            for ib in range(TB):
                                pe.wait_ge(s_a_free, (b * H + h) * TB + ib + 1)
                                keys = (ib + 1) * P
                                dst = ps[:, par * 4 + ib, :]
                                pe.matmul(dst[:, 0:keys], q1[:, bass.ds(h, 1), ib * P:keys].rearrange("p a n -> p (a n)"),
                                          k1[:, bass.ds(h, 1), 0:keys].rearrange("p a n -> p (a n)"), start=True, stop=False)
                                pe.matmul(dst[:, ib * P:keys], ident16[:, :], causal16[:, :], start=False,
                                          stop=True).then_inc(s_a_ps, 1)
                    pe.wait_ge(s_a_free, 2 * TB + (b + 1) * H * TB)
                    for t in range(TB):
                        mm = pe.transpose(ps[0:H, 0, :].bitcast(F16)[:, t * P:(t + 1) * P], negm[:, t, :], ident16[:, :])
                    mm.then_inc(s_nm_ps, 1)

                    def scores(p, n):
                        pe.wait_ge(s_mrow, 16 * (b + 1))
                        pe.wait_ge(s_dup, 32 * (b + 1))
                        pe.wait_ge(s_exp, n * 2 + 1)
                        for hh in range(2):
                            h = p * 2 + hh
                            for kb, (col, width) in REGION.items():
                                dst = ps_flat[:, hh * 1536 + col:hh * 1536 + col + width]

                                def part(t, a, z):
                                    return t[:, bass.ds(h, 1), a:z].rearrange("p a n -> p (a n)")

                                pe.matmul(dst, part(k1, kb * P, kb * P + P), part(q1, kb * P, T), start=True, stop=False)
                                pe.matmul(dst, part(k2, kb * P, kb * P + P), part(q2, kb * P, T), start=False, stop=False)
                                mm = pe.matmul(dst[:, 0:P], ident16[:, :], causal_t16[:, :], start=False, stop=True)
                            mm.then_inc(s_s_ps, 1)

                    def weighted(par, n):
                        pe.wait_ge(s_exp, n * 2 + 3)
                        pe.wait_ge(s_vst, n + 1)
                        pe.wait_ge(s_y, n + 1)
                        for bank in (6, 7):
                            for kb in range(TB):
                                col, width = REGION[kb]
                                for hh in range(2):
                                    r = slice(hh * D, (hh + 1) * D)
                                    mm = pe.matmul(ps[r, bank, kb * P:T], vst[:, par, kb, r] if bank == 6 else ones[:, :],
                                                   pt[:, par, hh, col:col + width], start=kb == 0, stop=kb == TB - 1)
                        mm.then_inc(s_pv, 1)

                    with pe.Fori(0, NP // 2) as it:
                        n = b * NP + it * 2
                        scores(it * 2, n)
                        scores(it * 2 + 1, n + 1)
                        weighted(0, n)
                        weighted(1, n + 1)
                    pe.wait_ge(s_y_l, (b + 1) * NP)
                    for p in range(NP):
                        mm = product(ps[:, 0, :], wp_h[:, p, :], wp_l[:, p, :], y_h[:, p, :], y_l[:, p, :],
                                     p == 0, p == NP - 1)
                    mm.then_inc(s_o_ps["att"], 1)
                    turn_back("att")

                ffn("ffn_a")
                attention()
                ffn("ffn_b")

        @block.vector
        def _(dve):
            d = nc.vector
            steps = [0]

            def link(ins):
                steps[0] += 1
                ins.then_inc(dve_step, 1)
                dve.wait_ge(dve_step, steps[0])

            d.memset(q1[64:128, :, :], 0.0).then_inc(s_a_free, 2 * TB)
            d.memset(k1[64:128, :, :], 0.0).then_inc(s_pv, 2)
            dve.wait_ge(s_a_free, 2 * TB)
            dve.wait_ge(s_pv, 2)
            d.memset(stats[:, :, :], 0.0).then_inc(s_sqsum, 4)
            d.memset(mv[:, :, :], 0.0).then_inc(s_y, 1)
            d.memset(ssv[:, :, :], 0.0).then_inc(s_exp, 1)
            d.memset(veps[:, :], 0.0).then_inc(s_x_new["ffn_a"], 1)
            d.memset(x_out[:, :, :], 0.0).then_inc(s_out, 16)
            link(d.memset(q1[96:100, :, :], 1.0))
            d.memset(k1[64:65, :, :], 1.0).then_inc(s_icol, 1)
            dve.wait_ge(s_icol, 2)
            d.tensor_copy(icol16[:, :], icol[:, :]).then_inc(s_icol, 1)
            dve.wait_ge(s_wload, 16 * 12)
            dve.wait_ge(s_unit, 64)
            link(d.tensor_scalar(wup, wld, QKV_UP, None, ALU.mult))
            link(d.tensor_copy(wqkv_h[:, :], wup))
            d.tensor_tensor(wqkv_l[:, :], wup, wqkv_h[:, :], ALU.subtract)
            link(d.tensor_scalar(wpu, wpl, W_UP, None, ALU.mult))
            link(d.tensor_copy(wp_h[:, :, :], wpu))
            d.tensor_tensor(wp_l[:, :, :], wpu, wp_h[:, :, :], ALU.subtract)
            d.tensor_scalar(b2half[:, :], b2c[:, :], 0.5, None, ALU.mult)
            d.tensor_scalar(sc_up[:, :], sc[:, :], W_UP, None, ALU.mult)
            d.tensor_scalar(qws[:, :], qw[:, :], 1.0 / (math.sqrt(D) * QKV_UP), None, ALU.mult)
            d.tensor_scalar(kws[:, :], kw[:, :], 1.0 / QKV_UP, None, ALU.mult)
            u3 = ub.rearrange("p (h n) -> p h n", h=H)
            q3 = uq.rearrange("p (h n) -> p h n", h=H)
            k3 = wld[:, HD:2 * HD].rearrange("p (h n) -> p h n", h=H)
            link(d.tensor_tensor(q3, u3, u3, ALU.mult))
            d.tensor_reduce(om_n[:, :], q3, AX.X, ALU.add).then_inc(s_usq, 1)
            dve.wait_ge(s_unorm, 1)
            link(d.tensor_scalar(un[:, :], un[:, :], U_EPS, None, ALU.max))
            link(d.reciprocal(un[:, :], un[:, :]))
            link(d.tensor_tensor(q3, u3, un[:, :].unsqueeze(2).broadcast_to([P, H, D]), ALU.mult))
            link(d.tensor_tensor(q3, q3, kwb[:, :].unsqueeze(1).broadcast_to([P, H, D]), ALU.mult))
            link(d.tensor_tensor(q3, q3, k3, ALU.mult))
            link(d.tensor_reduce(wu[:, :], q3, AX.X, ALU.add))
            link(d.tensor_scalar(wu[:, :], wu[:, :], W_UP / math.sqrt(D), None, ALU.mult))
            link(d.tensor_copy(wu_h[:, :], wu[:, :]))
            d.tensor_tensor(wu_l[:, :], wu[:, :], wu_h[:, :], ALU.subtract)
            link(d.tensor_scalar(om_e[:, :], om[:, :], -1.0, None, ALU.mult))
            d.tensor_tensor(om_n[:, :], om[:, :], om_e[:, :], ALU.min).then_inc(s_omn, 1)
            dve.wait_ge(s_oml, 2)
            link(d.scalar_tensor_tensor(om[:, :], om[:, :], 0.0, om_n[:, :], ALU.max, ALU.add))
            dve.wait_ge(s_const, 19)
            link(d.tensor_tensor(om[:, :], om[:, :], slopes[:, :], ALU.mult))
            dve.wait_ge(s_w12_ps, 2 * FB)
            d.tensor_scalar(w1s[:, :], ps[:, 0, :], W_UP, None, ALU.mult)
            link(d.tensor_scalar(w2s[:, :], ps[:, 1, :], W_UP, None, ALU.mult))
            link(d.memset(gt[:, :, :, :], 0.0))
            d.memset(ev[:, :, :], 0.0).then_inc(s_setup, 1)
            dve.wait_ge(s_setup, 1)
            before = steps[0]

            with dve.Fori(0, B) as b:
                in_batch = [0]

                def link(ins):
                    in_batch[0] += 1
                    ins.then_inc(dve_step, 1)
                    dve.wait_ge(dve_step, b * LINKS + before + in_batch[0])

                LINKS = 24

                def norm(name, src):
                    for t in range(TB):
                        ins = d.bn_stats(stats[:, t, :], src[:, t, :])
                    link(ins)
                    d.memset(veps[:, :], LN_EPS)
                    for t in range(TB):
                        ins = d.bn_aggr(mv[:, t, :], stats[:, t, :])
                    link(ins)
                    d.tensor_tensor(veps[:, :], mv[:, :, 1], veps[:, :], ALU.add).then_inc(s_var[name], 1)
                    dve.wait_ge(s_rstd[name], b + 1)
                    for t in range(TB):
                        d.tensor_scalar(z[:, t, :], src[:, t, :], mv[:, t, 0:1], rstd[:, t:t + 1], ALU.subtract,
                                        ALU.mult).then_inc(s_z[name], 1)
                    dve.wait_ge(s_zt_h[name], b + 1)
                    d.tensor_tensor(zt_l[:, :], ps[:, 0, :], zt_h[:, :], ALU.subtract).then_inc(s_zt_l[name], 1)

                def add_back(name, src, dst):
                    dve.wait_ge(s_ot_ps[name], b + 1)
                    d.tensor_tensor(dst[:, :, :].rearrange("p t c -> p (t c)"), ps[:, 1, :],
                                    src[:, :, :].rearrange("p t c -> p (t c)"), ALU.add).then_inc(s_x_new[name], 1)
                    dve.wait_ge(s_x_new[name], b + (2 if name == "ffn_a" else 1))

                def ffn(name, src, dst):
                    norm(name, src)
                    dve.wait_ge(s_sel_ps[name], b + 1)
                    for n in range(2):
                        d.tensor_copy(od[:, n, :], ps[:, 1, n * P:(n + 1) * P])
                    for r in range(FB):
                        rows = slice(r * RPT, (r + 1) * RPT)
                        d.tensor_copy(ev[rows, 0, r * P:(r + 1) * P], ps[rows, 1, 2 * P:3 * P])
                        dst2 = ev[rows, 1, :].rearrange("p (k r q) -> p k r q", k=FB, r=FB)[:, :, r, :]
                        ins = d.tensor_copy(dst2, ps[rows, 1, 3 * P:4 * P].rearrange("p (q k) -> p k q", k=FB))
                    ins.then_inc(s_ev[name], 1)
                    dve.wait_ge(s_m_ps[name], b + 1)
                    d.scalar_tensor_tensor(w1e[:, :], ps[:, 2, :], sc_up[:, :], w1s[:, :], ALU.mult, ALU.add)
                    link(d.scalar_tensor_tensor(w2e[:, :], ps[:, 3, :], sc_up[:, :], w2s[:, :], ALU.mult, ALU.add))
                    d.tensor_copy(w1_h[:, :], w1e[:, :])
                    link(d.tensor_copy(w2_h[:, :], w2e[:, :]))
                    d.tensor_tensor(w1_l[:, :], w1e[:, :], w1_h[:, :], ALU.subtract)
                    d.tensor_tensor(w2_l[:, :], w2e[:, :], w2_h[:, :], ALU.subtract).then_inc(s_wsplit[name], 1)
                    for r in range(FB):
                        dve.wait_ge(s_hid[name], b * FB + r + 1)
                        link(d.tensor_copy(hid_h[:, r, :], hid[:, r, :]))
                        d.tensor_tensor(hid_l[:, r, :], hid[:, r, :], hid_h[:, r, :],
                                        ALU.subtract).then_inc(s_hid_l[name], 1)
                    if name == "ffn_b":
                        dve.wait_ge(s_out, 16 * (b + 1))
                    add_back(name, src, dst)

                def attention():
                    norm("att", x_1)
                    for t in range(TB):
                        for c in range(4):
                            dve.wait_ge(s_sq, (b * TB + t) * 4 + c + 1)
                            d.tensor_reduce(ss[:, t, c * 8:(c + 1) * 8],
                                            sq[:, c, :].rearrange("p (h n) -> p h n", n=D), AX.X,
                                            ALU.add).then_inc(s_sqsum, 1)
                        dve.wait_ge(s_sqsum, (b * TB + t + 2) * 4)
                        d.tensor_scalar(ssv[:, t, :], ss[:, t, :], 1.0 / (D * QKV_UP * QKV_UP), RMS_EPS, ALU.mult,
                                        ALU.add).then_inc(s_ssv, 1)
                        dve.wait_ge(s_rs, b * TB + t + 1)
                        for c in range(4):
                            d.tensor_tensor(qkn[:, c // 2, t, (c % 2) * 512:(c % 2 + 1) * 512].rearrange("p (h n) -> p h n", n=D),
                                            ps[:, 1 + c, :].rearrange("p (h n) -> p h n", n=D),
                                            rs[:, t, c * 8:(c + 1) * 8].unsqueeze(2).broadcast_to([P, 8, D]),
                                            ALU.mult).then_inc(s_qkn, 1)
                    dve.wait_ge(s_gl_ps, (b + 1) * TB)
                    link(d.scalar_tensor_tensor(lg[:, :, :], ps[:, 7, 0:TB * H].rearrange("p (t h) -> p t h", h=H),
                                                1.0 / W_UP, rs[:, :, H:2 * H], ALU.mult, ALU.mult))
                    link(d.tensor_scalar(lgn[:, :, :], lg[:, :, :], -1.0, None, ALU.mult))
                    d.tensor_tensor(lga[:, :, :], lg[:, :, :], lgn[:, :, :], ALU.min).then_inc(s_lga, 1)
                    dve.wait_ge(s_lgl, b + 1)
                    link(d.scalar_tensor_tensor(sp_[:, :, :], lg[:, :, :], 0.0, lgl[:, :, :], ALU.max, ALU.add))
                    link(d.tensor_tensor(gate[:, :, :], sp_[:, :, :], om[:, :].unsqueeze(1).broadcast_to([P, TB, H]),
                                         ALU.mult))
                    link(d.tensor_tensor(jgate[:, :, :], gate[:, :, :],
                                         jcol[:, :].unsqueeze(2).broadcast_to([P, TB, H]), ALU.mult))
                    d.tensor_copy(gt[:, :, 0, :], gate[:, :, :])
                    link(d.tensor_copy(gt[:, :, 2, :], jgate[:, :, :]))
                    d.tensor_tensor(gt[:, :, 1, :], gate[:, :, :], gt[:, :, 0, :], ALU.subtract)
                    d.tensor_tensor(gt[:, :, 3, :], jgate[:, :, :], gt[:, :, 2, :], ALU.subtract).then_inc(s_gt, 1)
                    dve.wait_ge(s_gt_ps, b + 1)
                    d.tensor_copy(gtt[:, :], ps[0:4 * H, 5, :].bitcast(F16)[:, 0:T]).then_inc(s_gtt, 1)
                    for n in range(2 * NP):
                        for hh in range(2):
                            r = slice(hh * D, (hh + 1) * D)
                            h = 2 * (n // 2) + hh
                            dst, hi, w = ((q2[D:2 * D, h, :], q1, qws), (k2[0:D, h, :], k1, kws))[n % 2]
                            dve.wait_ge(s_hi, (b * 2 * NP + n) * 2 + hh + 1)
                            d.scalar_tensor_tensor(dst, ps[r, 1 + n % 4, :], w[r, :], hi[0:D, h, :], ALU.mult,
                                                   ALU.subtract).then_inc(s_lo, 1)
                    with dve.Fori(0, H // 2) as it:
                        for par in range(2):
                            h = it * 2 + par
                            for ib in range(TB):
                                dve.wait_ge(s_a_ps, (b * H + h) * TB + ib + 1)
                                d.tensor_reduce(negm[:, ib, bass.ds(h, 1)], ps[:, par * 4 + ib, 0:(ib + 1) * P], AX.X,
                                                ALU.max, negate=True).then_inc(s_a_free, 1)
                    dve.wait_ge(s_nm_ps, b + 1)
                    d.tensor_copy(nmt[:, :], ps[0:H, 0, :].bitcast(F16)[:, 0:T]).then_inc(s_nmt, 1)
                    with dve.Fori(0, NP) as p:
                        n = b * NP + p
                        dve.wait_ge(s_pv, n + 3)
                        d.reciprocal(rden[:, :], ps[:, 7, :]).then_inc(s_rden, 1)
                        dve.wait_ge(s_rden, n + 1)
                        d.tensor_tensor(yf[:, :], ps[:, 6, :], rden[:, :], ALU.mult).then_inc(s_y, 1)
                        dve.wait_ge(s_y, n + 2)
                        yh = y_h[:, bass.ds(p, 1), :].rearrange("p a n -> p (a n)")
                        yl = y_l[:, bass.ds(p, 1), :].rearrange("p a n -> p (a n)")
                        d.tensor_copy(yh, yf[:, :]).then_inc(s_y_h, 1)
                        dve.wait_ge(s_y_h, n + 1)
                        d.tensor_tensor(yl, yf[:, :], yh, ALU.subtract).then_inc(s_y_l, 1)
                    add_back("att", x_1, x_2)

                dve.wait_ge(s_x, 16 * (b + 1))
                ffn("ffn_a", x_in, x_1)
                attention()
                ffn("ffn_b", x_2, x_out)
                assert in_batch[0] == LINKS, in_batch


_INS = ["L0_attn_x", "L0_attn_Wq", "L0_attn_Wk", "L0_attn_Wv", "L0_attn_Wproj", "L0_attn_q_rms_w", "L0_attn_k_rms_w",
        "L0_attn_omega", "L0_attn_u", "L0_ffn_W1", "L0_ffn_b1", "L0_ffn_W2", "L0_ffn_b2", "L0_ffn_scale"]


def kernel(**inputs):
    import numpy as np
    import concourse.bacc as bacc
    from concourse.bass_utils import run_bass_kernel_spmd

    nc = bacc.Bacc("TRN2", target_bir_lowering=False, num_devices=1)
    arrays, args = {}, []
    for name in _INS:
        a = np.ascontiguousarray(inputs[name])
        a = a.reshape(a.shape or (1,))
        arrays[f"in_{name}"] = a
        args.append(nc.dram_tensor(f"in_{name}", a.shape, mybir.dt.from_np(a.dtype), kind="ExternalInput").ap())
    shape = arrays["in_L0_attn_x"].shape
    args.append(nc.dram_tensor("out_0", shape, F32, kind="ExternalOutput").ap())
    macaron(nc, *args)
    r = run_bass_kernel_spmd(nc, [arrays], core_ids=[0])
    return r.results[0]["out_0"]
```

```python
import math
from contextlib import ExitStack

import concourse.bass as bass
from concourse import mybir

ALU = mybir.AluOpType
ACT = mybir.ActivationFunctionType
AX = mybir.AxisListType
F32 = mybir.dt.float32
F16 = mybir.dt.float16

P = 128
LN_EPS = 1e-5
RMS_EPS = 1e-5
U_EPS = 1e-6
W_UP = 64.0
QKV_UP = 16.0
MASKED = -60000.0
EXP_SET = "natural_log_exp_and_others"

LAST, THIS, NEXT = -1, 0, 1


def operands(half, whose):
    return {
        "qk": [("qk", half, t, whose) for t in range(4)],
        "qkn": [("qkn", half, t, whose) for t in range(4)],
        "gl": ("gl", half, whose), "gate": ("gate", half, whose), "gr": ("gr", half, whose),
        "t": [("t", p, whose) for p in range(4 * half, 4 * half + 4)],
        "a": [("a", h, whose) for h in range(8 * half, 8 * half + 8)],
        "nm": ("nm", half, whose),
    }


H0, H1 = operands(0, NEXT), operands(1, THIS)
V = [("v", t, NEXT) for t in range(4)]


def ffn_stage(stage, n):
    return (stage, n, NEXT if n == "a" else LAST)


SLOTS = [
    ([H1["qk"][0], ffn_stage("ln1", "a")], [H1["qk"][1], H1["qkn"][0]]),
    ([("attback", LAST), H1["qk"][2], H1["qkn"][1], ffn_stage("ln2", "a")], [H1["qk"][3], H1["qkn"][2], ffn_stage("ln1", "c")]),
    ([H1["gl"], ffn_stage("zt", "a"), ffn_stage("sel", "a"), H1["qkn"][3]], [("shift", THIS), H1["t"][0], H1["gate"]]),
    ([H1["t"][1], ffn_stage("ln2", "c")], [ffn_stage("m", "a"), H1["gr"], H1["t"][2]]),
    ([H1["t"][3]], [ffn_stage("h", "a"), H1["a"][0]]),
    ([H1["a"][1], H1["a"][2]], [H1["a"][3], ffn_stage("out", "a")]),
    ([H1["a"][4], H1["a"][5]], [H1["a"][6], H1["a"][7], ffn_stage("back", "a"), ("ln1", "att", NEXT)]),
    ([H1["nm"], ffn_stage("zt", "c")], [ffn_stage("sel", "c"), ("ln2", "att", NEXT)]),
    ([("zt", "att", NEXT), H0["qk"][0]], [H0["qk"][1], H0["qkn"][0]]),
    ([H0["qk"][2], H0["qkn"][1]], [H0["qk"][3], H0["qkn"][2], ffn_stage("m", "c")]),
    ([H0["gl"], H0["qkn"][3]], [H0["t"][0], H0["gate"], H0["t"][1]]),
    ([H0["gr"], H0["t"][2]], [H0["t"][3], ffn_stage("h", "c")]),
    ([H0["a"][0]], [H0["a"][1], ffn_stage("out", "c")]),
    ([H0["a"][2]], [H0["a"][3], ffn_stage("back", "c")]),
    ([H0["a"][4]], [H0["a"][5]]),
    ([H0["a"][6]], [H0["a"][7]]),
]


def iteration():
    out = []
    for h, (first, second) in enumerate(SLOTS):
        out.append(("s", h, THIS))
        if h >= 3 and h % 2:
            out.append(("yt", (h - 3) // 2, THIS))
        if h >= 4 and h % 2 == 0:
            out.append(("wp", (h - 4) // 2, THIS))
        out += first
        if h:
            out += [("pv", h - 1, THIS), ("yn", h - 1, THIS)]
        out += second
    return out + [H0["nm"], ("pv", 15, THIS), ("yn", 15, THIS), ("wp", 6, THIS), V[0], V[1], ("yt", 7, THIS), V[2], V[3],
                  ("wp", 7, THIS)]


BODY = iteration()
PART = {
    "lead": [s for s in BODY if s[-1] == NEXT],
    "first": [s for s in BODY if s[-1] != LAST],
    "body": BODY,
    "final": [s for s in BODY if s[-1] != NEXT],
    "tail": [s for s in BODY if s[-1] == LAST],
}
UNITS = {"zt": 1, "sel": 2, "m": 2, "h": 4, "out": 1, "back": 1, "qk": 2, "gl": 1, "gr": 1, "t": 2, "a": 3, "nm": 1, "v": 2,
         "yt": 1, "attback": 1}
RING = (5, 6, 7)


def units(part):
    return sum(UNITS.get(s[0], 0) for s in PART[part])


def slopes_of(heads):
    start = 2.0 ** (-2.0 ** (-(math.log2(heads) - 3)))
    return [start * start ** i for i in range(heads)]


def macaron(nc: bass.Bass, x, Wq, Wk, Wv, Wproj, q_rms_w, k_rms_w, omega, u, W1, b1, W2, b2, scale, out):
    B, T, C = x.shape
    H, D = u.shape
    HD = H * D
    F = W1.shape[0]
    TB = T // P
    FB = F // P
    NP = H // 2
    HH = H // 2
    RPT = P // FB
    GROW = 64
    MROW = 96
    assert C == P and T == 512 and F == 512 and D == 64 and H == 16 and B >= 3
    assert units("body") % len(RING) == 0
    REGION = {0: (0, 512), 1: (512, 384), 3: (896, 128), 2: (1024, 256)}
    SCOLS = 1280
    SBANK = [((0,), 0, 512), ((1, 3), 512, 512), ((2,), 1024, 256)]

    with ExitStack() as ctx:
        def sb(name, shape, dt=F32):
            return ctx.enter_context(nc.sbuf_tensor(name, shape, dt))

        def sem(name):
            return ctx.enter_context(nc.semaphore(name))

        ps = ctx.enter_context(nc.psum_tensor("ps", [P, 8, 512], F32))
        Y_BANK, ACC_BANK = 3, 4

        ident = sb("ident", [P, P])
        ident16 = sb("ident16", [P, P], F16)
        causal16 = sb("causal16", [P, P], F16)
        causal_t16 = sb("causal_t16", [P, P], F16)
        rms_eps = sb("rms_eps", [P, 1])
        half = sb("half", [P, H])
        ones = sb("ones", [P, 1])
        sel = sb("sel", [P, 4, P])
        jcol = sb("jcol", [P, TB])
        w1s = sb("w1s", [P, F])
        w2s = sb("w2s", [P, F])
        wqkv_h = sb("wqkv_h", [P, 3 * HD], F16)
        wqkv_l = sb("wqkv_l", [P, 3 * HD], F16)
        wp_h = sb("wp_h", [P, NP, C], F16)
        wp_l = sb("wp_l", [P, NP, C], F16)
        wu = sb("wu", [P, H])
        wu_h = sb("wu_h", [P, H], F16)
        wu_l = sb("wu_l", [P, H], F16)
        b1c = sb("b1c", [P, FB])
        b2c = sb("b2c", [P, 1])
        b2half = sb("b2half", [P, 1])
        sc = sb("sc", [P, 1])
        sc_up = sb("sc_up", [P, 1])
        qw = sb("qw", [P, 1])
        kw = sb("kw", [P, 1])
        qws = sb("qws", [P, 1])
        kws = sb("kws", [P, 1])
        om = sb("om", [P, H])
        om_e = sb("om_e", [P, H])
        om_n = sb("om_n", [P, H])
        slopes = sb("slopes", [P, H])
        un = sb("un", [P, H])
        kwb = sb("kwb", [P, D])
        x_in = sb("x_in", [P, TB, C])
        x_1 = sb("x_1", [P, TB, C])
        x_1old = sb("x_1old", [P, TB, C])
        x_2 = sb("x_2", [P, TB, C])
        x_out = sb("x_out", [P, TB, C])
        NORMS = ("a", "att", "c")
        stats = {n: sb(f"stats_{n}", [P, TB, 6]) for n in NORMS}
        mv = {n: sb(f"mv_{n}", [P, TB, 2]) for n in NORMS}
        veps = {n: sb(f"veps_{n}", [P, TB]) for n in NORMS}
        lnv = {n: sb(f"lnv_{n}", [P, TB]) for n in NORMS}
        rstd = {n: sb(f"rstd_{n}", [P, TB]) for n in NORMS}
        z = {n: sb(f"z_{n}", [P, TB, C]) for n in NORMS}
        zt_h = {n: sb(f"zt_h_{n}", [P, T], F16) for n in NORMS}
        zt_l = {n: sb(f"zt_l_{n}", [P, T], F16) for n in NORMS}
        o_ffn = sb("o_ffn", [P, T])
        o_att = sb("o_att", [P, T])
        od = sb("od", [P, 2, P])
        ev = sb("ev", [P, 2, F])
        weff = sb("weff", [P, 2, F])
        w_h = sb("w_h", [P, 2, F], F16)
        w_l = sb("w_l", [P, 2, F], F16)
        hid = sb("hid", [P, FB, T])
        hid_h = sb("hid_h", [P, FB, T], F16)
        hid_l = sb("hid_l", [P, FB, T], F16)
        sq = sb("sq", [P, 2, 2, 512])
        ss = sb("ss", [P, TB, 2 * HH])
        ssl = sb("ssl", [P, TB, 2 * HH])
        rs = sb("rs", [P, TB, 2 * HH])
        qkn = sb("qkn", [P, 2, TB, HH * D])
        v = sb("v", [P, TB, H, D + 1])
        q1 = sb("q1", [P, H, T], F16)
        k1 = sb("k1", [P, H, T], F16)
        q2 = sb("q2", [P, H, T], F16)
        k2 = sb("k2", [P, H, T], F16)
        lg = sb("lg", [P, TB, HH])
        lgn = sb("lgn", [P, TB, HH])
        lga = sb("lga", [P, TB, HH])
        lge = sb("lge", [P, TB, HH])
        lgl = sb("lgl", [P, TB, HH])
        sp_ = sb("sp_", [P, TB, HH])
        gate = sb("gate", [P, TB, HH])
        jgate = sb("jgate", [P, TB, HH])
        gt = sb("gt", [P, TB, 4, HH], F16)
        gtt = sb("gtt", [4 * HH, T], F16)
        negm = sb("negm", [P, TB, H], F16)
        nmt = sb("nmt", [HH, T], F16)
        pt = sb("pt", [P, 2, SCOLS])
        rden = sb("rden", [P, TB])
        ytok = sb("ytok", [P, 2, TB, 2 * D])
        y_h = sb("y_h", [P, 2, T], F16)
        y_l = sb("y_l", [P, 2, T], F16)

        qkn_flat = qkn[:, :, :, :].rearrange("p a t n -> p (a t n)")
        v_flat = v[:, :, :, :].rearrange("p t h n -> p (t h n)")
        wld = qkn_flat[:, 0:3 * HD]
        uq = qkn_flat[:, 3 * HD:4 * HD]
        wup = v_flat[:, 0:3 * HD]
        ub = v_flat[:, 3 * HD:4 * HD]
        wpl = hid[:, 0:2, :].rearrange("p a n -> p (a n)").rearrange("p (a n) -> p a n", a=NP)
        wpu = hid[:, 2:4, :].rearrange("p a n -> p (a n)").rearrange("p (a n) -> p a n", a=NP)
        w1ld = sq[:, 0, 0, :].rearrange("p (a n) -> p a n", a=FB)
        w2ld = sq[:, 0, 1, :]
        icol = weff[:, 0, :]
        icol16 = w_h[:, 0, :]

        s_wload = sem("s_wload")
        s_unit = sem("s_unit")
        s_const = sem("s_const")
        s_icol = sem("s_icol")
        s_rows = sem("s_rows")
        s_w12_ps = sem("s_w12_ps")
        s_setup = sem("s_setup")
        s_usq = sem("s_usq")
        s_unorm = sem("s_unorm")
        s_omn = sem("s_omn")
        s_oml = sem("s_oml")
        dve_step = sem("dve_step")
        pool_step = sem("pool_step")
        work_full = [sem(f"work_full{i}") for i in range(len(RING))]
        work_taken = [sem(f"work_taken{i}") for i in range(len(RING))]
        s_x = sem("s_x")
        s_out = sem("s_out")
        s_dup = sem("s_dup")
        s_grow = sem("s_grow")
        s_mrow = sem("s_mrow")
        s_var = {n: sem(f"s_var_{n}") for n in NORMS}
        s_lnv = {n: sem(f"s_lnv_{n}") for n in NORMS}
        s_rstd = {n: sem(f"s_rstd_{n}") for n in NORMS}
        s_z = {n: sem(f"s_z_{n}") for n in NORMS}
        s_zt_h = {n: sem(f"s_zt_h_{n}") for n in NORMS}
        s_wsplit = {n: sem(f"s_wsplit_{n}") for n in ("a", "c")}
        s_hid_l = {n: sem(f"s_hid_l_{n}") for n in ("a", "c")}
        s_sq = sem("s_sq")
        s_sqsum = sem("s_sqsum")
        s_ssl = sem("s_ssl")
        s_rs = sem("s_rs")
        s_qkn = sem("s_qkn")
        s_lga = sem("s_lga")
        s_lge = sem("s_lge")
        s_lgl = sem("s_lgl")
        s_gt = sem("s_gt")
        s_hi = sem("s_hi")
        s_s_ps = sem("s_s_ps")
        s_exp = sem("s_exp")
        s_pv = sem("s_pv")
        s_rden = sem("s_rden")
        s_y = sem("s_y")
        s_y_h = sem("s_y_h")
        s_acc = sem("s_acc")
        s_acc_taken = sem("s_acc_taken")

        block = ctx.enter_context(nc.Block())

        def row_of(a):
            return a.rearrange("(o n) -> o n", o=1)

        class Part:

            def __init__(self, part, before, rounds=0):
                self.part, self.before, self.rounds = part, before, rounds
                self.at, n = {}, 0
                for s in PART[part]:
                    self.at[s] = n
                    n += UNITS.get(s[0], 0)

            def unit(self, stage, i=0):
                n = self.before + self.at[stage] + i
                return n % len(RING), n // len(RING) + self.rounds

            def bank(self, stage, i=0):
                return ps[:, RING[self.unit(stage, i)[0]], :]

            def room(self, eng, stage, i=0):
                r, uses = self.unit(stage, i)
                if not (isinstance(uses, int) and uses == 0):
                    eng.wait_ge(work_taken[r], uses)

            def full(self, eng, stage, i=0):
                r, uses = self.unit(stage, i)
                eng.wait_ge(work_full[r], uses + 1)

            def taken(self, eng, stage, i=0, then=None):
                r, uses = self.unit(stage, i)
                if then is None or self.unit(then)[0] != r:
                    eng.wait_ge(work_taken[r], uses + 1)

            def filled_by(self, ins, stage, i=0):
                ins.then_inc(work_full[self.unit(stage, i)[0]], 1)

            def taken_by(self, ins, stage, i=0):
                ins.then_inc(work_taken[self.unit(stage, i)[0]], 1)

        def run(eng, do, at_part=None):
            def stages(part, b):
                for s in PART[part.part]:
                    if s[0] in do:
                        do[s[0]](part, s, b + s[-1], *s[1:-1])

            n = units("lead")
            stages(Part("lead", 0), -1)
            stages(Part("first", n), 0)
            n += units("first")
            if at_part:
                at_part("body")
            with eng.Fori(1, B - 1) as b:
                stages(Part("body", n, (b - 1) * (units("body") // len(RING))), b)
            if at_part:
                at_part("final")
            n += (B - 2) * units("body")
            stages(Part("final", n), B - 1)
            stages(Part("tail", n + units("final")), B)

        @block.sync
        def _(sp):
            for i, w in enumerate((Wq, Wk, Wv)):
                sp.dma_start(wld[:, i * HD:(i + 1) * HD], w).then_inc(s_wload, 16)
            sp.dma_start(wpl, Wproj.rearrange("(a p) n -> p a n", p=P)).then_inc(s_wload, 16)
            sp.dma_start(w1ld, W1.rearrange("(a p) n -> p a n", p=P)).then_inc(s_wload, 16)
            sp.dma_start(w2ld, W2).then_inc(s_wload, 16)
            sp.dma_start(b1c[:, :], b1.rearrange("(a p) -> p a", p=P),
                         allow_slow_non_contiguous=True).then_inc(s_wload, 16)
            sp.dma_start(b2c[:, :], b2.rearrange("(p o) -> p o", o=1)).then_inc(s_wload, 16)
            sp.dma_start(sc[:, :], row_of(scale).broadcast_to([P, 1])).then_inc(s_wload, 16)
            sp.dma_start(om[:, :], row_of(omega).broadcast_to([P, H])).then_inc(s_wload, 16)
            sp.dma_start(kwb[:, :], row_of(k_rms_w).broadcast_to([P, D])).then_inc(s_wload, 16)
            sp.dma_start(ub, row_of(u.rearrange("h d -> (h d)")).broadcast_to([P, HD])).then_inc(s_wload, 16)
            for n in range(2):
                sp.dma_start(qw[n * D:(n + 1) * D, :], q_rms_w.rearrange("(p o) -> p o", o=1)).then_inc(s_unit, 16)
                sp.dma_start(kw[n * D:(n + 1) * D, :], k_rms_w.rearrange("(p o) -> p o", o=1)).then_inc(s_unit, 16)
            sp.wait_ge(s_icol, 3)
            for h in range(H):
                sp.dma_start(q1[GROW:GROW + 2, h, :], icol16[0:2, :]).then_inc(s_rows, 16)

            def load_x(part, s, b, n):
                if n == "a":
                    if not (isinstance(b, int) and b == 0):
                        sp.wait_ge(s_var["att"], b)
                    sp.dma_start(x_in[:, :, :], x[b].rearrange("(t p) c -> p t c", p=P) if isinstance(b, int) else
                                 x[bass.ds(b, 1)].rearrange("o (t p) c -> p (o t) c", p=P)).then_inc(s_x, 16)

            def gate_rows(part, s, b, hf):
                part.taken(sp, s)
                sp.wait_ge(s_hi, b * 2 * H + (hf + 1) * H)
                for r in range(4):
                    sp.dma_start(k1[GROW + r:GROW + r + 1, hf * HH:(hf + 1) * HH, :],
                                 gtt[r * HH:(r + 1) * HH, :]).then_inc(s_grow, 16)

            def copy_parts(part, s, b, hf):
                hs = slice(hf * HH, (hf + 1) * HH)
                sp.dma_start(q2[0:D, hs, :], q1[0:D, hs, :]).then_inc(s_dup, 16)
                sp.dma_start(k2[D:2 * D, hs, :], k1[0:D, hs, :]).then_inc(s_dup, 16)

            def max_rows(part, s, b, hf):
                part.taken(sp, s)
                sp.dma_start(q1[MROW:MROW + 1, hf * HH:(hf + 1) * HH, :], nmt[:, :]).then_inc(s_mrow, 16)

            def rows_and_parts(part, s, b, hf):
                gate_rows(part, s, b, hf)
                copy_parts(part, s, b, hf)

            def store(part, s, b, n):
                if n == "c":
                    part.taken(sp, s)
                    sp.dma_start(out[b].rearrange("(t p) c -> p t c", p=P) if isinstance(b, int) else
                                 out[bass.ds(b, 1)].rearrange("o (t p) c -> p (o t) c", p=P),
                                 x_out[:, :, :]).then_inc(s_out, 16)

            run(sp, {"ln1": load_x, "gr": rows_and_parts, "nm": max_rows, "back": store})
            sp.wait_ge(s_out, 16 * B)

        @block.gpsimd
        def _(pool):
            g = nc.gpsimd
            g.memset(ident[:, :], 0.0).then_inc(s_const, 1)
            g.memset(ident16[:, :], 0.0).then_inc(s_const, 1)
            g.memset(causal16[:, :], 0.0).then_inc(s_const, 1)
            g.memset(causal_t16[:, :], 0.0).then_inc(s_const, 1)
            g.memset(sel[:, :, :], 0.0).then_inc(s_const, 1)
            g.iota(jcol[:, :], [[P, TB]], base=-(T // 2), channel_multiplier=1,
                   allow_small_or_imprecise_dtypes=True).then_inc(s_const, 1)
            g.iota(icol, [[-1, T]], base=T // 2, channel_multiplier=0,
                   allow_small_or_imprecise_dtypes=True).then_inc(s_icol, 1)
            for t, n in ((rms_eps, RMS_EPS), (half, 0.5), (ones, 1.0)):
                g.memset(t[:, :], n).then_inc(s_const, 1)
            for h, s in enumerate(slopes_of(H)):
                last = g.memset(slopes[:, h:h + 1], s)
            last.then_inc(s_const, 1)
            pool.wait_ge(s_const, 5)
            for m in (ident, ident16):
                g.affine_select(out=m[:, :], in_=m[:, :], compare_op=ALU.not_equal, fill=1.0, base=0,
                                pattern=[[-1, P]], channel_multiplier=1).then_inc(s_const, 1)
            g.affine_select(out=causal16[:, :], in_=causal16[:, :], compare_op=ALU.is_ge, fill=MASKED, base=0,
                            pattern=[[-1, P]], channel_multiplier=1).then_inc(s_const, 1)
            g.affine_select(out=causal_t16[:, :], in_=causal_t16[:, :], compare_op=ALU.is_ge, fill=MASKED, base=0,
                            pattern=[[1, P]], channel_multiplier=-1).then_inc(s_const, 1)
            for n, first in enumerate((2, 10, 1, 9)):
                s = sel[:, n, :].rearrange("p (r e) -> p r e", r=FB)
                g.affine_select(out=s, in_=s, compare_op=ALU.not_equal, fill=1.0, base=-first,
                                pattern=[[-2, FB], [1000, RPT]], channel_multiplier=1).then_inc(s_const, 1)
            pool.wait_ge(s_const, 18)
            pool.wait_ge(s_usq, 1)
            g.tensor_tensor(un[:, :], om_n[:, :], half[:, :], ALU.pow).then_inc(s_unorm, 1)
            pool.wait_ge(s_setup, 1)

            def split_weights(part, s, b, n):
                for i in range(2):
                    part.taken(pool, s, i)
                    g.tensor_tensor(w_h[:, i, :], weff[:, i, :], ones[:, :].broadcast_to([P, F]), ALU.mult).then_inc(pool_step, 1)
                    steps["n"] += 1
                    pool.wait_ge(pool_step, step_count(b, n))
                    g.tensor_tensor(w_l[:, i, :], weff[:, i, :], w_h[:, i, :], ALU.subtract).then_inc(s_wsplit[n], 1)

            def split_hidden(part, s, b, n):
                for r in range(FB):
                    part.taken(pool, s, r)
                    g.tensor_tensor(hid_h[:, r, :], hid[:, r, :], ones[:, :].broadcast_to([P, T]), ALU.mult).then_inc(pool_step, 1)
                    steps["n"] += 1
                    pool.wait_ge(pool_step, step_count(b, n))
                    g.tensor_tensor(hid_l[:, r, :], hid[:, r, :], hid_h[:, r, :], ALU.subtract).then_inc(s_hid_l[n], 1)

            def over_rms(part, s, b, hf, t):
                pool.wait_ge(s_rs, (b * 2 + hf) * TB + t + 1)
                for j in range(2):
                    qk = qkn[:, j, t, :].rearrange("p (h n) -> p h n", n=D)
                    g.tensor_tensor(qk, qk, rs[:, t, j * HH:(j + 1) * HH].unsqueeze(2).broadcast_to([P, HH, D]),
                                    ALU.mult).then_inc(s_qkn, 1)

            steps = {"n": 0, "start": None}
            PER_ITERATION = 2 * (2 + FB)

            def step_count(b, n):
                if isinstance(b, int):
                    return steps["n"]
                return (b - (2 if n == "a" else 0)) * PER_ITERATION + steps["n"]

            def at_part(part):
                if part == "body":
                    steps["start"] = steps["n"]
                else:
                    assert steps["n"] - steps["start"] == PER_ITERATION
                    steps["n"] = steps["start"] + (B - 2) * PER_ITERATION

            run(pool, {"qkn": over_rms, "m": split_weights, "h": split_hidden}, at_part)

        @block.scalar
        def _(act):
            a = nc.scalar
            act.preload_act_table_set(EXP_SET)
            act.wait_ge(s_omn, 1)
            a.activation(om_e[:, :], om_n[:, :], ACT.Exp).then_inc(s_oml, 1)
            act.wait_ge(s_oml, 1)
            a.activation(om_n[:, :], om_e[:, :], ACT.Ln, bias=1.0).then_inc(s_oml, 1)
            act.wait_ge(s_setup, 1)

            def zt_hi(part, s, b, n):
                part.full(act, s)
                a.activation(zt_h[n][:, :], part.bank(s), ACT.Copy).then_inc(s_zt_h[n], 1)

            def gelu(part, s, b, n):
                for r in range(FB):
                    part.full(act, s, r)
                    part.taken_by(a.activation(hid[:, r, :], part.bank(s, r), ACT.Gelu, bias=b1c[:, r:r + 1],
                                               scale=1.0 / W_UP), s, r)
                act.preload_act_table_set(EXP_SET)

            def ffn_out(part, s, b, n):
                part.full(act, s)
                part.taken_by(a.activation(o_ffn[:, :], part.bank(s), ACT.Identity, bias=b2half[:, :],
                                           scale=0.5 / W_UP), s)

            def take_qk(part, s, b, hf, t):
                blk = (b * 2 + hf) * TB + t
                for j in range(2):
                    part.full(act, s, j)
                    if not (isinstance(blk, int) and blk < 2):
                        act.wait_ge(s_sqsum, (blk - 2) * 2 + j + 1)
                    a.activation(sq[:, t % 2, j, :], part.bank(s, j), ACT.Square).then_inc(s_sq, 1)
                    part.taken_by(a.activation(qkn[:, j, t, :], part.bank(s, j), ACT.Copy), s, j)

            def inverse_rms(part, s, b, hf, t):
                blk = (b * 2 + hf) * TB + t
                act.wait_ge(s_sqsum, blk * 2 + 2)
                a.activation(ssl[:, t, :], ss[:, t, :], ACT.Ln, bias=rms_eps[:, :],
                             scale=1.0 / (D * QKV_UP * QKV_UP)).then_inc(s_ssl, 1)
                act.wait_ge(s_ssl, blk + 1)
                a.activation(rs[:, t, :], ssl[:, t, :], ACT.Exp, scale=-0.5).then_inc(s_rs, 1)

            def inverse_root(part, s, b, n):
                act.wait_ge(s_var[n], b + 1)
                a.activation(lnv[n][:, :], veps[n][:, :], ACT.Ln).then_inc(s_lnv[n], 1)
                act.wait_ge(s_lnv[n], b + 1)
                a.activation(rstd[n][:, :], lnv[n][:, :], ACT.Exp, scale=-0.5).then_inc(s_rstd[n], 1)

            def gate_softplus(part, s, b, hf):
                act.wait_ge(s_lga, b * 2 + hf + 1)
                a.activation(lge[:, :, :], lga[:, :, :], ACT.Exp).then_inc(s_lge, 1)
                act.wait_ge(s_lge, b * 2 + hf + 1)
                a.activation(lgl[:, :, :], lge[:, :, :], ACT.Ln, bias=1.0).then_inc(s_lgl, 1)

            def hi_parts(part, s, b, p):
                for j, (dst, w) in enumerate(((q1, qws), (k1, kws))):
                    part.full(act, s, j)
                    for hh in range(2):
                        r = slice(hh * D, (hh + 1) * D)
                        a.activation(dst[0:D, 2 * p + hh, :], part.bank(s, j)[r, :], ACT.Identity,
                                     scale=w[r, :]).then_inc(s_hi, 1)

            def take_v(part, s, b, t):
                for j in range(2):
                    part.full(act, s, j)
                    part.taken_by(a.activation(v[:, t, j * HH:(j + 1) * HH, 0:D],
                                               part.bank(s, j).rearrange("p (h n) -> p h n", n=D), ACT.Copy), s, j)

            def exponentials(part, s, b, h):
                n = b * H + h
                if not (isinstance(n, int) and n < 2):
                    act.wait_ge(s_pv, n - 1)
                for j, (_, col, width) in enumerate(SBANK):
                    act.wait_ge(s_s_ps, n * 3 + j + 1)
                    a.activation(pt[:, h % 2, col:col + width], ps[:, j, 0:width], ACT.Exp).then_inc(s_exp, 1)

            def y_hi(part, s, b, p):
                part.full(act, s)
                a.activation(y_h[:, p % 2, :], part.bank(s), ACT.Copy).then_inc(s_y_h, 1)

            def take_projection(part, s, b):
                act.wait_ge(s_acc, b + 1)
                a.activation(o_att[:, :], ps[:, ACC_BANK, :], ACT.Identity,
                             scale=1.0 / (W_UP * QKV_UP)).then_inc(s_acc_taken, 1)

            run(act, {"ln1": inverse_root, "qkn": inverse_rms, "zt": zt_hi, "h": gelu, "out": ffn_out, "qk": take_qk, "gate": gate_softplus, "t": hi_parts,
                      "v": take_v, "s": exponentials, "yt": y_hi, "attback": take_projection})

        @block.tensor
        def _(pe):
            pe.wait_ge(s_const, 18)
            pe.wait_ge(s_wload, 16 * 12)
            for r in range(FB):
                pe.transpose(ps[:, 0, r * P:(r + 1) * P], w1ld[:, r, :], ident[:, :]).then_inc(s_w12_ps, 1)
            for r in range(FB):
                pe.transpose(ps[:, 1, r * P:(r + 1) * P], w2ld[:, r * P:(r + 1) * P], ident[:, :]).then_inc(s_w12_ps, 1)
            pe.wait_ge(s_setup, 1)
            pe.wait_ge(s_rows, 16 * H)

            def product(dst, ah, al, bh, bl, first=True, last=True):
                pe.matmul(dst, ah, bh, start=first, stop=False)
                pe.matmul(dst, ah, bl, start=False, stop=False)
                return pe.matmul(dst, al, bh, start=False, stop=last)

            def turn(part, s, src):
                part.room(pe, s)
                for t in range(TB):
                    mm = pe.transpose(part.bank(s)[:, t * P:(t + 1) * P], src(t), ident[:, :])
                part.filled_by(mm, s)

            def zt(part, s, b, n):
                pe.wait_ge(s_z[n], (b + 1) * TB)
                turn(part, s, lambda t: z[n][:, t, :])

            def adapter_vectors(part, s, b, n):
                for i in range(2):
                    part.room(pe, s, i)
                    for f in range(2):
                        mm = pe.matmul(part.bank(s, i)[:, f * P:(f + 1) * P], sel[:, 2 * i + f, :], z[n][:, 0, :],
                                       start=True, stop=True)
                    part.filled_by(mm, s, i)

            def adapter_blocks(part, s, b, n):
                for i in range(2):
                    part.taken(pe, ("sel", *s[1:]), i, then=s)
                for i in range(2):
                    part.room(pe, s, i)
                    part.filled_by(pe.matmul(part.bank(s, i), od[:, i, :], ev[:, i, :], start=True, stop=True), s, i)

            def hidden(part, s, b, n):
                pe.wait_ge(s_wsplit[n], (b + 1) * 2)
                part.taken(pe, ("zt", *s[1:]), then=s)
                for r in range(FB):
                    c = slice(r * P, (r + 1) * P)
                    part.room(pe, s, r)
                    part.filled_by(product(part.bank(s, r), w_h[:, 0, c], w_l[:, 0, c], zt_h[n][:, :], zt_l[n][:, :]), s, r)

            def ffn_out(part, s, b, n):
                part.room(pe, s)
                for r in range(FB):
                    pe.wait_ge(s_hid_l[n], b * FB + r + 1)
                    c = slice(r * P, (r + 1) * P)
                    mm = product(part.bank(s), w_h[:, 1, c], w_l[:, 1, c], hid_h[:, r, :], hid_l[:, r, :], r == 0, r == FB - 1)
                part.filled_by(mm, s)

            def ffn_back(part, s, b, n):
                part.taken(pe, ("out", *s[1:]), then=s)
                turn(part, s, lambda t: o_ffn[:, t * P:(t + 1) * P])

            def attention_back(part, s, b):
                pe.wait_ge(s_acc_taken, b + 1)
                turn(part, s, lambda t: o_att[:, t * P:(t + 1) * P])

            def project_qk(part, s, b, hf, t):
                if (hf, t) == (0, 0):
                    part.taken(pe, ("zt", "att", s[-1]), then=s)
                for j in range(2):
                    w = slice(j * HD + hf * 512, j * HD + hf * 512 + 512)
                    c = slice(t * P, (t + 1) * P)
                    part.room(pe, s, j)
                    part.filled_by(product(part.bank(s, j), zt_h["att"][:, c], zt_l["att"][:, c], wqkv_h[:, w],
                                           wqkv_l[:, w]), s, j)

            def project_v(part, s, b, t):
                for j in range(2):
                    w = slice(2 * HD + j * 512, 2 * HD + j * 512 + 512)
                    c = slice(t * P, (t + 1) * P)
                    part.room(pe, s, j)
                    part.filled_by(product(part.bank(s, j), zt_h["att"][:, c], zt_l["att"][:, c], wqkv_h[:, w],
                                           wqkv_l[:, w]), s, j)

            def gate_logits(part, s, b, hf):
                w = slice(hf * HH, (hf + 1) * HH)
                part.room(pe, s)
                for t in range(TB):
                    c = slice(t * P, (t + 1) * P)
                    mm = product(part.bank(s)[:, t * HH:(t + 1) * HH], zt_h["att"][:, c], zt_l["att"][:, c], wu_h[:, w],
                                 wu_l[:, w])
                part.filled_by(mm, s)

            def gate_rows(part, s, b, hf):
                pe.wait_ge(s_gt, b * 2 + hf + 1)
                part.room(pe, s)
                for t in range(TB):
                    mm = pe.transpose(part.bank(s)[0:4 * HH, :].bitcast(F16)[:, t * P:(t + 1) * P],
                                      gt[:, t, :, :].rearrange("p r h -> p (r h)"), ident16[:, :])
                part.filled_by(mm, s)

            def turn_heads(part, s, b, p):
                pe.wait_ge(s_qkn, (b * 2 + p // 4 + 1) * TB * 2)
                for j in range(2):
                    part.room(pe, s, j)
                    for t in range(TB):
                        mm = pe.transpose(part.bank(s, j)[:, t * P:(t + 1) * P],
                                          qkn[:, j, t, (p % 4) * P:(p % 4 + 1) * P], ident[:, :])
                    part.filled_by(mm, s, j)

            def max_scores(part, s, b, h):
                pe.wait_ge(s_grow, (b * 2 + h // HH + 1) * 64)
                pe.wait_ge(s_hi, b * 2 * H + (h // 2 + 1) * 4)
                for i, blocks in enumerate(((3,), (2, 0), (1,))):
                    part.room(pe, s, i)
                    for ib in blocks:
                        keys = (ib + 1) * P
                        col = 384 if len(blocks) == 2 and ib == 0 else 0
                        dst = part.bank(s, i)[:, col:col + keys]
                        pe.matmul(dst, q1[0:MROW, h, ib * P:keys], k1[0:MROW, h, 0:keys], start=True, stop=False)
                        mm = pe.matmul(dst[:, ib * P:keys], ident16[:, :], causal16[:, :], start=False, stop=True)
                    part.filled_by(mm, s, i)

            def turn_max(part, s, b, hf):
                part.taken(pe, ("a", hf * HH + HH - 1, s[-1]), 2, then=s)
                part.room(pe, s)
                for t in range(TB):
                    mm = pe.transpose(part.bank(s)[0:HH, :].bitcast(F16)[:, t * P:(t + 1) * P],
                                      negm[:, t, hf * HH:(hf + 1) * HH], ident16[:, :])
                part.filled_by(mm, s)

            def scores(part, s, b, h):
                n = b * H + h
                if h % HH == 0:
                    pe.wait_ge(s_mrow, (b * 2 + h // HH + 1) * 16)
                    pe.wait_ge(s_dup, (b * 2 + h // HH + 1) * 32)
                for j, (blocks, first, _) in enumerate(SBANK):
                    if not (isinstance(n, int) and n == 0):
                        pe.wait_ge(s_exp, (n - 1) * 3 + j + 1)
                    for kb in blocks:
                        col, width = REGION[kb]
                        dst = ps[:, j, col - first:col - first + width]
                        keys = slice(kb * P, kb * P + P)
                        pe.matmul(dst, k1[:, h, keys], q1[:, h, kb * P:T], start=True, stop=False)
                        pe.matmul(dst, k2[:, h, keys], q2[:, h, kb * P:T], start=False, stop=False)
                        mm = pe.matmul(dst[:, 0:P], ident16[:, :], causal_t16[:, :], start=False, stop=True)
                    mm.then_inc(s_s_ps, 1)

            def weighted(part, s, b, h):
                n = b * H + h
                pe.wait_ge(s_exp, (n + 1) * 3)
                if not (isinstance(n, int) and n == 0):
                    pe.wait_ge(s_y, n)
                for ib in range(TB):
                    for kb in range(ib + 1):
                        col = REGION[kb][0] + (ib - kb) * P
                        mm = pe.matmul(ps[:, Y_BANK, ib * (D + 1):(ib + 1) * (D + 1)], pt[:, h % 2, col:col + P],
                                       v[:, kb, h, :], start=kb == 0, stop=kb == ib)
                mm.then_inc(s_pv, 1)

            def turn_y(part, s, b, p):
                pe.wait_ge(s_y, b * H + 2 * p + 2)
                turn(part, s, lambda t: ytok[:, p % 2, t, :])

            def project_out(part, s, b, p):
                part.taken(pe, ("yt", *s[1:]))
                if p == 0 and not (isinstance(b, int) and b == 0):
                    pe.wait_ge(s_acc_taken, b)
                mm = product(ps[:, ACC_BANK, :], wp_h[:, p, :], wp_l[:, p, :], y_h[:, p % 2, :], y_l[:, p % 2, :], p == 0,
                             p == NP - 1)
                if p == NP - 1:
                    mm.then_inc(s_acc, 1)

            run(pe, {"zt": zt, "sel": adapter_vectors, "m": adapter_blocks, "h": hidden, "out": ffn_out, "back": ffn_back,
                     "attback": attention_back, "qk": project_qk, "v": project_v, "gl": gate_logits, "gr": gate_rows,
                     "t": turn_heads, "a": max_scores, "nm": turn_max, "s": scores, "pv": weighted, "yt": turn_y,
                     "wp": project_out})

        @block.vector
        def _(dve):
            d = nc.vector
            steps = {"n": 0, "start": None}
            PER_ITERATION = 16

            def link(ins, rounds=0):
                steps["n"] += 1
                ins.then_inc(dve_step, 1)
                dve.wait_ge(dve_step, rounds * PER_ITERATION + steps["n"])

            def at_part(part):
                if part == "body":
                    steps["start"] = steps["n"]
                else:
                    assert steps["n"] - steps["start"] == PER_ITERATION, steps
                    steps["n"] = steps["start"] + (B - 2) * PER_ITERATION

            link(d.memset(q1[D:P, :, :], 0.0))
            link(d.memset(k1[D:P, :, :], 0.0))
            link(d.memset(q1[GROW:GROW + 4, :, :], 1.0))
            d.memset(k1[MROW:MROW + 1, :, :], 1.0).then_inc(s_icol, 1)
            dve.wait_ge(s_icol, 2)
            d.tensor_copy(icol16, icol).then_inc(s_icol, 1)
            dve.wait_ge(s_wload, 16 * 12)
            dve.wait_ge(s_unit, 64)
            link(d.tensor_scalar(wup, wld, QKV_UP, None, ALU.mult))
            link(d.tensor_copy(wqkv_h[:, :], wup))
            d.tensor_tensor(wqkv_l[:, :], wup, wqkv_h[:, :], ALU.subtract)
            link(d.tensor_scalar(wpu, wpl, W_UP, None, ALU.mult))
            link(d.tensor_copy(wp_h[:, :, :], wpu))
            d.tensor_tensor(wp_l[:, :, :], wpu, wp_h[:, :, :], ALU.subtract)
            d.tensor_scalar(b2half[:, :], b2c[:, :], 0.5, None, ALU.mult)
            d.tensor_scalar(sc_up[:, :], sc[:, :], W_UP, None, ALU.mult)
            d.tensor_scalar(qws[:, :], qw[:, :], 1.0 / (math.sqrt(D) * QKV_UP), None, ALU.mult)
            d.tensor_scalar(kws[:, :], kw[:, :], 1.0 / QKV_UP, None, ALU.mult)
            u3 = ub.rearrange("p (h n) -> p h n", h=H)
            q3 = uq.rearrange("p (h n) -> p h n", h=H)
            k3 = wld[:, HD:2 * HD].rearrange("p (h n) -> p h n", h=H)
            link(d.tensor_tensor(q3, u3, u3, ALU.mult))
            d.tensor_reduce(om_n[:, :], q3, AX.X, ALU.add).then_inc(s_usq, 1)
            dve.wait_ge(s_unorm, 1)
            link(d.tensor_scalar(un[:, :], un[:, :], U_EPS, None, ALU.max))
            link(d.reciprocal(un[:, :], un[:, :]))
            link(d.tensor_tensor(q3, u3, un[:, :].unsqueeze(2).broadcast_to([P, H, D]), ALU.mult))
            link(d.tensor_tensor(q3, q3, kwb[:, :].unsqueeze(1).broadcast_to([P, H, D]), ALU.mult))
            link(d.tensor_tensor(q3, q3, k3, ALU.mult))
            link(d.tensor_reduce(wu[:, :], q3, AX.X, ALU.add))
            link(d.tensor_scalar(wu[:, :], wu[:, :], W_UP / math.sqrt(D), None, ALU.mult))
            link(d.tensor_copy(wu_h[:, :], wu[:, :]))
            d.tensor_tensor(wu_l[:, :], wu[:, :], wu_h[:, :], ALU.subtract)
            link(d.tensor_scalar(om_e[:, :], om[:, :], -1.0, None, ALU.mult))
            d.tensor_tensor(om_n[:, :], om[:, :], om_e[:, :], ALU.min).then_inc(s_omn, 1)
            dve.wait_ge(s_oml, 2)
            link(d.scalar_tensor_tensor(om[:, :], om[:, :], 0.0, om_n[:, :], ALU.max, ALU.add))
            dve.wait_ge(s_const, 18)
            link(d.tensor_tensor(om[:, :], om[:, :], slopes[:, :], ALU.mult))
            dve.wait_ge(s_w12_ps, 2 * FB)
            d.tensor_scalar(w1s[:, :], ps[:, 0, :], W_UP, None, ALU.mult)
            link(d.tensor_scalar(w2s[:, :], ps[:, 1, :], W_UP, None, ALU.mult))
            link(d.memset(v[:, :, :, D:D + 1], 1.0))
            dve.wait_ge(s_rows, 16 * H)
            d.memset(ev[:, :, :], 0.0).then_inc(s_setup, 1)
            dve.wait_ge(s_setup, 1)

            def statistics(part, s, b, n):
                src = {"a": x_in, "att": x_1, "c": x_2}[n]
                if n == "a":
                    dve.wait_ge(s_x, (b + 1) * 16)
                r = rounds(b, s)
                for t in range(TB):
                    ins = d.bn_stats(stats[n][:, t, :], src[:, t, :])
                link(ins, r)
                d.memset(veps[n][:, :], LN_EPS)
                for t in range(TB):
                    ins = d.bn_aggr(mv[n][:, t, :], stats[n][:, t, :])
                link(ins, r)
                d.tensor_tensor(veps[n][:, :], mv[n][:, :, 1], veps[n][:, :], ALU.add).then_inc(s_var[n], 1)

            def rounds(b, s):
                return 0 if isinstance(b, int) else b - s[-1] - 1

            def normalize(part, s, b, n):
                src = {"a": x_in, "att": x_1, "c": x_2}[n]
                dve.wait_ge(s_rstd[n], b + 1)
                for t in range(TB):
                    d.tensor_scalar(z[n][:, t, :], src[:, t, :], mv[n][:, t, 0:1], rstd[n][:, t:t + 1], ALU.subtract,
                                    ALU.mult).then_inc(s_z[n], 1)

            def zt_lo(part, s, b, n):
                part.full(dve, s)
                dve.wait_ge(s_zt_h[n], b + 1)
                part.taken_by(d.tensor_tensor(zt_l[n][:, :], part.bank(s), zt_h[n][:, :], ALU.subtract), s)

            def adapter_factors(part, s, b, n):
                part.full(dve, s, 0)
                part.taken_by(d.tensor_copy(od[:, :, :].rearrange("p a n -> p (a n)"), part.bank(s, 0)[:, 0:2 * P]), s, 0)
                part.full(dve, s, 1)
                for r in range(FB):
                    rows = slice(r * RPT, (r + 1) * RPT)
                    d.tensor_copy(ev[rows, 0, r * P:(r + 1) * P], part.bank(s, 1)[rows, 0:P])
                    dst = ev[rows, 1, :].rearrange("p (k r q) -> p k r q", k=FB, r=FB)[:, :, r, :]
                    ins = d.tensor_copy(dst, part.bank(s, 1)[rows, P:2 * P].rearrange("p (q k) -> p k q", k=FB))
                part.taken_by(ins, s, 1)

            def adapted_weights(part, s, b, n):
                for i, w in enumerate((w1s, w2s)):
                    part.full(dve, s, i)
                    part.taken_by(d.scalar_tensor_tensor(weff[:, i, :], part.bank(s, i), sc_up[:, :], w[:, :], ALU.mult,
                                                         ALU.add), s, i)

            def add_ffn(part, s, b, n):
                src, dst = {"a": (x_in, x_1), "c": (x_2, x_out)}[n]
                if n == "c" and not (isinstance(b, int) and b == 0):
                    dve.wait_ge(s_out, 16 * b)
                add(part, s, src, dst)

            def add(part, s, src, dst):
                part.full(dve, s)
                part.taken_by(d.tensor_tensor(dst[:, :, :].rearrange("p t c -> p (t c)"), part.bank(s),
                                              src[:, :, :].rearrange("p t c -> p (t c)"), ALU.add), s)
                part.taken(dve, s)

            def add_attention(part, s, b):
                add(part, s, x_1old, x_2)

            def keep_x1(part, s, b):
                d.tensor_copy(x_1old[:, :, :], x_1[:, :, :])

            def square_sums(part, s, b, hf, t):
                blk = (b * 2 + hf) * TB + t
                for j in range(2):
                    dve.wait_ge(s_sq, blk * 2 + j + 1)
                    d.tensor_reduce(ss[:, t, j * HH:(j + 1) * HH], sq[:, t % 2, j, :].rearrange("p (h n) -> p h n", n=D), AX.X,
                                    ALU.add).then_inc(s_sqsum, 1)

            def take_logits(part, s, b, hf):
                r = rounds(b, s)
                part.full(dve, s)
                dve.wait_ge(s_rs, (b * 2 + hf + 1) * TB)
                part.taken_by(d.scalar_tensor_tensor(lg[:, :, :], part.bank(s)[:, 0:TB * HH].rearrange("p (t h) -> p t h", h=HH),
                                                     1.0 / W_UP, rs[:, :, HH:2 * HH], ALU.mult, ALU.mult), s)
                part.taken(dve, s)
                link(d.tensor_scalar(lgn[:, :, :], lg[:, :, :], -1.0, None, ALU.mult), r)
                d.tensor_tensor(lga[:, :, :], lg[:, :, :], lgn[:, :, :], ALU.min).then_inc(s_lga, 1)

            def gates(part, s, b, hf):
                r = rounds(b, s)
                dve.wait_ge(s_lgl, b * 2 + hf + 1)
                link(d.scalar_tensor_tensor(sp_[:, :, :], lg[:, :, :], 0.0, lgl[:, :, :], ALU.max, ALU.add), r)
                link(d.tensor_tensor(gate[:, :, :], sp_[:, :, :],
                                     om[:, hf * HH:(hf + 1) * HH].unsqueeze(1).broadcast_to([P, TB, HH]), ALU.mult), r)
                link(d.tensor_tensor(jgate[:, :, :], gate[:, :, :], jcol[:, :].unsqueeze(2).broadcast_to([P, TB, HH]),
                                     ALU.mult), r)
                d.tensor_copy(gt[:, :, 0, :], gate[:, :, :])
                link(d.tensor_copy(gt[:, :, 2, :], jgate[:, :, :]), r)
                d.tensor_tensor(gt[:, :, 1, :], gate[:, :, :], gt[:, :, 0, :], ALU.subtract)
                d.tensor_tensor(gt[:, :, 3, :], jgate[:, :, :], gt[:, :, 2, :], ALU.subtract).then_inc(s_gt, 1)

            def take_gate_rows(part, s, b, hf):
                part.full(dve, s)
                g = b * 2 + hf
                if not (isinstance(g, int) and g == 0):
                    dve.wait_ge(s_grow, g * 64)
                part.taken_by(d.tensor_copy(gtt[:, :], part.bank(s)[0:4 * HH, :].bitcast(F16)[:, 0:T]), s)

            def lo_parts(part, s, b, p):
                for j, w in enumerate((qws, kws)):
                    part.full(dve, s, j)
                    for hh in range(2):
                        h = 2 * p + hh
                        r = slice(hh * D, (hh + 1) * D)
                        dst, hi = ((q2[D:2 * D, h, :], q1), (k2[0:D, h, :], k1))[j]
                        dve.wait_ge(s_hi, b * 2 * H + p * 4 + j * 2 + hh + 1)
                        ins = d.scalar_tensor_tensor(dst, part.bank(s, j)[r, :], w[r, :], hi[0:D, h, :], ALU.mult, ALU.subtract)
                    part.taken_by(ins, s, j)

            def maxima(part, s, b, h):
                for i, blocks in enumerate(((3,), (2, 0), (1,))):
                    part.full(dve, s, i)
                    for ib in blocks:
                        col = 384 if len(blocks) == 2 and ib == 0 else 0
                        ins = d.tensor_reduce(negm[:, ib, h:h + 1], part.bank(s, i)[:, col:col + (ib + 1) * P], AX.X, ALU.max,
                                              negate=True)
                    part.taken_by(ins, s, i)

            def take_max_rows(part, s, b, hf):
                part.full(dve, s)
                g = b * 2 + hf
                if not (isinstance(g, int) and g == 0):
                    dve.wait_ge(s_mrow, g * 16)
                part.taken_by(d.tensor_copy(nmt[:, :], part.bank(s)[0:HH, :].bitcast(F16)[:, 0:T]), s)

            def over_sums(part, s, b, h):
                n = b * H + h
                y = ps[:, Y_BANK, 0:TB * (D + 1)].rearrange("p (t n) -> p t n", n=D + 1)
                dve.wait_ge(s_pv, n + 1)
                d.reciprocal(rden[:, :], y[:, :, D]).then_inc(s_rden, 1)
                dve.wait_ge(s_rden, n + 1)
                d.tensor_tensor(ytok[:, (h // 2) % 2, :, (h % 2) * D:(h % 2 + 1) * D], y[:, :, 0:D],
                                rden[:, :].unsqueeze(2).broadcast_to([P, TB, D]), ALU.mult).then_inc(s_y, 1)

            def y_lo(part, s, b, p):
                part.full(dve, s)
                dve.wait_ge(s_y_h, b * NP + p + 1)
                part.taken_by(d.tensor_tensor(y_l[:, p % 2, :], part.bank(s), y_h[:, p % 2, :], ALU.subtract), s)

            run(dve, {"ln1": statistics, "ln2": normalize, "zt": zt_lo, "sel": adapter_factors, "m": adapted_weights,
                      "back": add_ffn, "attback": add_attention, "shift": keep_x1, "qk": square_sums,
                      "gl": take_logits, "gate": gates, "gr": take_gate_rows, "t": lo_parts, "a": maxima,
                      "nm": take_max_rows, "yn": over_sums, "yt": y_lo}, at_part)


_INS = ["L0_attn_x", "L0_attn_Wq", "L0_attn_Wk", "L0_attn_Wv", "L0_attn_Wproj", "L0_attn_q_rms_w", "L0_attn_k_rms_w",
        "L0_attn_omega", "L0_attn_u", "L0_ffn_W1", "L0_ffn_b1", "L0_ffn_W2", "L0_ffn_b2", "L0_ffn_scale"]


def kernel(**inputs):
    import numpy as np
    import concourse.bacc as bacc
    from concourse.bass_utils import run_bass_kernel_spmd

    nc = bacc.Bacc("TRN2", target_bir_lowering=False, num_devices=1)
    arrays, args = {}, []
    for name in _INS:
        a = np.ascontiguousarray(inputs[name])
        a = a.reshape(a.shape or (1,))
        arrays[f"in_{name}"] = a
        args.append(nc.dram_tensor(f"in_{name}", a.shape, mybir.dt.from_np(a.dtype), kind="ExternalInput").ap())
    shape = arrays["in_L0_attn_x"].shape
    args.append(nc.dram_tensor("out_0", shape, F32, kind="ExternalOutput").ap())
    macaron(nc, *args)
    r = run_bass_kernel_spmd(nc, [arrays], core_ids=[0])
    return r.results[0]["out_0"]
```

```python
import math
from contextlib import ExitStack

import concourse.bass as bass
from concourse import mybir

ALU = mybir.AluOpType
ACT = mybir.ActivationFunctionType
AX = mybir.AxisListType
F32 = mybir.dt.float32
F16 = mybir.dt.float16

P = 128
LN_EPS = 1e-5
RMS_EPS = 1e-5
U_EPS = 1e-6
W_UP = 64.0
QKV_UP = 16.0
MASKED = -60000.0
EXP_SET = "natural_log_exp_and_others"

LAST, THIS, NEXT = -1, 0, 1


SLOTS = [
    [("s", 0, THIS), ("ln1", "a", NEXT), ("pl", 0, THIS), ("gr", 1, THIS), ("pv", 15, LAST), ("ln2", "a", NEXT),
     ("t", 7, THIS), ("v", 1, 0, THIS)],
    [("s", 1, THIS), ("pl", 1, THIS), ("pv", 0, THIS), ("sel", "a", NEXT), ("v", 1, 1, THIS), ("v", 1, 2, THIS),
     ("v", 1, 3, THIS)],
    [("s", 2, THIS), ("pl", 2, THIS), ("rows", 1, THIS), ("m", "a", NEXT), ("pv", 1, THIS), ("zt", "a", NEXT),
     ("yt", 7, LAST)],
    [("s", 3, THIS), ("pl", 3, THIS), ("a", 8, THIS), ("pv", 2, THIS), ("a", 9, THIS), ("h", "a", NEXT),
     ("wp", 3, LAST)],
    [("s", 4, THIS), ("pl", 4, THIS), ("a", 10, THIS), ("pv", 3, THIS), ("out", "a", NEXT), ("ln1", "c", LAST),
     ("a", 11, THIS), ("yt", 0, THIS), ("yt", 1, THIS)],
    [("s", 5, THIS), ("pl", 5, THIS), ("a", 12, THIS), ("wp", 0, THIS), ("back", "a", NEXT), ("pv", 4, THIS),
     ("ln1", "att", NEXT), ("a", 13, THIS)],
    [("s", 6, THIS), ("pl", 6, THIS), ("ln2", "att", NEXT), ("a", 14, THIS), ("pv", 5, THIS),
     ("zt", "att", NEXT)],
    [("s", 7, THIS), ("pl", 7, THIS), ("a", 15, THIS), ("ln2", "c", LAST), ("qk", 0, 0, NEXT), ("nm", 1, THIS),
     ("qk", 0, 1, NEXT), ("sel", "c", LAST), ("qkn", 0, 0, NEXT), ("qk", 0, 2, NEXT), ("pv", 6, THIS),
     ("qkn", 0, 1, NEXT), ("qk", 0, 3, NEXT), ("yt", 2, THIS), ("qkn", 0, 2, NEXT), ("zt", "c", LAST),
     ("qkn", 0, 3, NEXT)],
    [("s", 8, THIS), ("pl", 8, THIS), ("pv", 7, THIS), ("gl", 0, NEXT), ("m", "c", LAST), ("v", 0, 0, NEXT),
     ("yt", 3, THIS), ("v", 0, 1, NEXT), ("gate", 0, NEXT), ("t", 0, NEXT), ("t", 1, NEXT)],
    [("s", 9, THIS), ("pl", 9, THIS), ("gr", 0, NEXT), ("pv", 8, THIS), ("t", 2, NEXT), ("t", 3, NEXT),
     ("h", "c", LAST), ("v", 0, 2, NEXT), ("v", 0, 3, NEXT)],
    [("s", 10, THIS), ("pl", 10, THIS), ("wp", 1, THIS), ("pv", 9, THIS), ("out", "c", LAST), ("rows", 0, NEXT),
     ("a", 0, NEXT)],
    [("s", 11, THIS), ("pl", 11, THIS), ("a", 1, NEXT), ("pv", 10, THIS), ("a", 2, NEXT)],
    [("s", 12, THIS), ("pl", 12, THIS), ("a", 3, NEXT), ("qk", 1, 0, NEXT), ("back", "c", LAST),
     ("qk", 1, 1, NEXT), ("yt", 4, THIS), ("pv", 11, THIS), ("qk", 1, 2, NEXT), ("qkn", 1, 0, NEXT),
     ("a", 4, NEXT)],
    [("s", 13, THIS), ("pl", 13, THIS), ("qkn", 1, 1, NEXT), ("pv", 12, THIS), ("a", 5, NEXT),
     ("qk", 1, 3, NEXT), ("yt", 5, THIS), ("a", 6, NEXT), ("qkn", 1, 2, NEXT), ("qkn", 1, 3, NEXT)],
    [("s", 14, THIS), ("pl", 14, THIS), ("gl", 1, NEXT), ("pv", 13, THIS), ("a", 7, NEXT), ("gate", 1, NEXT)],
    [("s", 15, THIS), ("wp", 2, THIS), ("nm", 0, NEXT), ("yt", 6, THIS), ("pl", 15, THIS), ("t", 4, NEXT),
     ("t", 5, NEXT), ("pv", 14, THIS), ("t", 6, NEXT)],
]


BODY = sum(SLOTS, [])
PART = {
    "lead": [s for s in BODY if s[-1] == NEXT],
    "first": [s for s in BODY if s[-1] != LAST],
    "body": BODY,
    "final": [s for s in BODY if s[-1] != NEXT],
    "tail": [s for s in BODY if s[-1] == LAST],
}
PART["lead"].insert(PART["lead"].index(("m", "a", NEXT)), ("weights", NEXT))
PART["lead"].insert(PART["lead"].index(("h", "a", NEXT)) + 1, ("prepare", NEXT))
PART["lead"].insert(PART["lead"].index(("qk", 0, 0, NEXT)), ("prepared", NEXT))
UNITS = {"zt": 2, "sel": 2, "m": 2, "h": 4, "out": 1, "back": 1, "qk": 2, "gl": 1, "gr": 1, "t": 2, "a": 3, "nm": 1, "v": 1,
         "yt": 1, "wp": 1}
RING = (4, 5, 6, 7)


def units(part):
    return sum(UNITS.get(s[0], 0) for s in PART[part])


def slopes_of(heads):
    start = 2.0 ** (-2.0 ** (-(math.log2(heads) - 3)))
    return [start * start ** i for i in range(heads)]


def macaron(nc: bass.Bass, x, Wq, Wk, Wv, Wproj, q_rms_w, k_rms_w, omega, u, W1, b1, W2, b2, scale, out):
    B, T, C = x.shape
    H, D = u.shape
    HD = H * D
    F = W1.shape[0]
    TB = T // P
    FB = F // P
    NP = H // 2
    HH = H // 2
    RPT = P // FB
    GROW = 64
    MROW = 96
    assert C == P and T == 512 and F == 512 and D == 64 and H == 16 and B >= 3
    assert units("body") % len(RING) == 0
    REGION = {0: (0, 512), 1: (512, 384), 3: (896, 128), 2: (1024, 256)}
    SCOLS = 1280
    SBANK = [((0,), 0, 512), ((1, 3), 512, 512), ((2,), 1024, 256)]

    with ExitStack() as ctx:
        def sb(name, shape, dt=F32):
            return ctx.enter_context(nc.sbuf_tensor(name, shape, dt))

        def sem(name):
            return ctx.enter_context(nc.semaphore(name))

        ps = ctx.enter_context(nc.psum_tensor("ps", [P, 8, 512], F32))
        Y_BANK = 3

        ident = sb("ident", [P, P])
        ident16 = sb("ident16", [P, P], F16)
        causal16 = sb("causal16", [P, P], F16)
        causal_t16 = sb("causal_t16", [P, P], F16)
        rms_eps = sb("rms_eps", [P, 1])
        half = sb("half", [P, H])
        sel = sb("sel", [P, 4, P])
        jcol = sb("jcol", [P, TB])
        w1s = sb("w1s", [P, F])
        w2s = sb("w2s", [P, F])
        wqkv_h = sb("wqkv_h", [P, 3 * HD], F16)
        wqkv_l = sb("wqkv_l", [P, 3 * HD], F16)
        wp_h = sb("wp_h", [P, NP, C], F16)
        wp_l = sb("wp_l", [P, NP, C], F16)
        wu = sb("wu", [P, H])
        wu_h = sb("wu_h", [P, H], F16)
        wu_l = sb("wu_l", [P, H], F16)
        b1c = sb("b1c", [P, FB])
        b2c = sb("b2c", [P, 1])
        b2half = sb("b2half", [P, 1])
        sc = sb("sc", [P, 1])
        sc_up = sb("sc_up", [P, 1])
        qw = sb("qw", [P, 1])
        kw = sb("kw", [P, 1])
        qws = sb("qws", [P, 1])
        kws = sb("kws", [P, 1])
        om = sb("om", [P, H])
        om_e = sb("om_e", [P, H])
        om_n = sb("om_n", [P, H])
        slopes = sb("slopes", [P, H])
        un = sb("un", [P, H])
        kwb = sb("kwb", [P, D])
        x_in = sb("x_in", [P, TB, C])
        x_1 = sb("x_1", [P, TB, C])
        x_att = sb("x_att", [P, TB, C])
        x_2 = sb("x_2", [P, TB, C])
        x_out = sb("x_out", [P, TB, C])
        NORMS = ("a", "att", "c")
        stats = {n: sb(f"stats_{n}", [P, TB, 6]) for n in NORMS}
        mv = {n: sb(f"mv_{n}", [P, TB, 2]) for n in NORMS}
        veps = {n: sb(f"veps_{n}", [P, TB]) for n in NORMS}
        lnv = {n: sb(f"lnv_{n}", [P, TB]) for n in NORMS}
        rstd = {n: sb(f"rstd_{n}", [P, TB]) for n in NORMS}
        z = {n: sb(f"z_{n}", [P, TB, C]) for n in ("a", "att")}
        zt_h = {n: sb(f"zt_h_{n}", [P, T], F16) for n in ("a", "att")}
        zt_l = {n: sb(f"zt_l_{n}", [P, T], F16) for n in ("a", "att")}
        z["c"], zt_h["c"], zt_l["c"] = z["a"], zt_h["a"], zt_l["a"]
        o_ffn = sb("o_ffn", [P, T])
        od = sb("od", [P, 2, P])
        ev = sb("ev", [P, 2, F])
        weff = sb("weff", [P, 2, F])
        w_h = sb("w_h", [P, 2, F], F16)
        w_l = sb("w_l", [P, 2, F], F16)
        hid = sb("hid", [P, 2, T])
        hid_h = sb("hid_h", [P, FB, T], F16)
        hid_l = sb("hid_l", [P, FB, T], F16)
        sq = sb("sq", [P, 2, 2, 512])
        ss = sb("ss", [P, TB, 2 * HH])
        ssl = sb("ssl", [P, TB, 2 * HH])
        rs = sb("rs", [P, TB, 2 * HH])
        qkn = sb("qkn", [P, 2, HH // 2, TB * P])
        v_buf = sb("v_buf", [P, 2 * TB * H * (D + 1)], F16)
        v_hl = v_buf[:, :].rearrange("p (a t h n) -> p a t h n", a=2, t=TB, h=H)
        q1 = sb("q1", [P, H, T], F16)
        k1 = sb("k1", [P, H, T], F16)
        q2 = sb("q2", [P, H, T], F16)
        k2 = sb("k2", [P, H, T], F16)
        lg = sb("lg", [P, TB, HH])
        lgn = sb("lgn", [P, TB, HH])
        lga = sb("lga", [P, TB, HH])
        lge = sb("lge", [P, TB, HH])
        lgl = sb("lgl", [P, TB, HH])
        softplus = sb("softplus", [P, TB, HH])
        gate = sb("gate", [P, TB, HH])
        jgate = sb("jgate", [P, TB, HH])
        gt = sb("gt", [P, TB, 4, HH], F16)
        gtt = sb("gtt", [4 * HH, T], F16)
        negm = sb("negm", [P, TB, H], F16)
        nmt = sb("nmt", [HH, T], F16)
        pt = sb("pt", [P, 2, SCOLS])
        pt_h = sb("pt_h", [P, 2, SCOLS], F16)
        pt_l = sb("pt_l", [P, 2, SCOLS], F16)
        rden = sb("rden", [P, TB])
        ytok = sb("ytok", [P, 2, TB, 2 * D])
        y_h = sb("y_h", [P, 2, T], F16)
        y_l = sb("y_l", [P, 2, T], F16)

        qkn16 = qkn[:, :, :, :].bitcast(F16)
        qkn_flat = qkn[:, :, :, :].rearrange("p a t n -> p (a t n)")
        v_flat = v_buf[:, 0:2 * 4 * HD].bitcast(F32)
        k2_flat = k2[:, 0:8, :].rearrange("p h n -> p (h n)").bitcast(F32)
        wld = qkn_flat[:, 0:3 * HD]
        uk = qkn_flat[:, 3 * HD:4 * HD]
        usq = v_flat[:, 0:HD]
        ub = v_flat[:, 3 * HD:4 * HD]
        wpl = k2_flat[:, 0:NP * C].rearrange("p (a n) -> p a n", a=NP)
        w1ld = sq[:, 0, 0, :].rearrange("p (a n) -> p a n", a=FB)
        w2ld = sq[:, 0, 1, :]
        icol = weff[:, 0, :]
        rows16 = y_h[:, 0, :]

        s_wffn = sem("s_wffn")
        s_wload = sem("s_wload")
        s_unit = sem("s_unit")
        s_const = sem("s_const")
        s_icol = sem("s_icol")
        s_rows16 = sem("s_rows16")
        s_whi = sem("s_whi")
        s_uk = sem("s_uk")
        s_rows = sem("s_rows")
        s_w12_ps = sem("s_w12_ps")
        s_setup = sem("s_setup")
        s_zeros = sem("s_zeros")
        s_prepared = sem("s_prepared")
        s_usq = sem("s_usq")
        s_unorm = sem("s_unorm")
        s_omn = sem("s_omn")
        s_oml = sem("s_oml")
        dve_step = sem("dve_step")
        work_full = [sem(f"work_full{i}") for i in range(len(RING))]
        work_taken = [sem(f"work_taken{i}") for i in range(len(RING))]
        s_x = sem("s_x")
        s_out = sem("s_out")
        s_dup = sem("s_dup")
        s_grow = sem("s_grow")
        s_mrow = sem("s_mrow")
        s_var = {n: sem(f"s_var_{n}") for n in NORMS}
        s_lnv = {n: sem(f"s_lnv_{n}") for n in NORMS}
        s_rstd = {n: sem(f"s_rstd_{n}") for n in NORMS}
        s_z = {n: sem(f"s_z_{n}") for n in NORMS}
        s_zt_h = {n: sem(f"s_zt_h_{n}") for n in NORMS}
        s_w_h = {n: sem(f"s_w_h_{n}") for n in ("a", "c")}
        s_w_l = {n: sem(f"s_w_l_{n}") for n in ("a", "c")}
        s_hid_h = {n: sem(f"s_hid_h_{n}") for n in ("a", "c")}
        s_hid_l = {n: sem(f"s_hid_l_{n}") for n in ("a", "c")}
        s_sq = sem("s_sq")
        s_sqsum = sem("s_sqsum")
        s_ssl = sem("s_ssl")
        s_rs = sem("s_rs")
        s_qkn = sem("s_qkn")
        s_lga = sem("s_lga")
        s_lge = sem("s_lge")
        s_lgl = sem("s_lgl")
        s_gt = sem("s_gt")
        s_hi = sem("s_hi")
        s_s_ps = sem("s_s_ps")
        s_v_h = sem("s_v_h")
        s_exp = sem("s_exp")
        s_pt_l = sem("s_pt_l")
        s_pv = sem("s_pv")
        s_rden = sem("s_rden")
        s_y = sem("s_y")
        s_y_h = sem("s_y_h")

        block = ctx.enter_context(nc.Block())

        def row_of(a):
            return a.rearrange("(o n) -> o n", o=1)

        class Part:

            def __init__(self, part, before, rounds=0):
                self.part, self.before, self.rounds = part, before, rounds
                self.at, n = {}, 0
                for s in PART[part]:
                    self.at[s] = n
                    n += UNITS.get(s[0], 0)

            def unit(self, stage, i=0):
                n = self.before + self.at[stage] + i
                return n % len(RING), n // len(RING) + self.rounds

            def bank(self, stage, i=0):
                return ps[:, RING[self.unit(stage, i)[0]], :]

            def room(self, eng, stage, i=0):
                r, uses = self.unit(stage, i)
                if not (isinstance(uses, int) and uses == 0):
                    eng.wait_ge(work_taken[r], uses)

            def full(self, eng, stage, i=0):
                r, uses = self.unit(stage, i)
                eng.wait_ge(work_full[r], uses + 1)

            def taken(self, eng, stage, i=0, then=None):
                r, uses = self.unit(stage, i)
                if then is None or self.unit(then)[0] != r:
                    eng.wait_ge(work_taken[r], uses + 1)

            def filled_by(self, ins, stage, i=0):
                ins.then_inc(work_full[self.unit(stage, i)[0]], 1)

            def taken_by(self, ins, stage, i=0):
                ins.then_inc(work_taken[self.unit(stage, i)[0]], 1)

        def run(eng, do, at_part=None):
            def stages(part, b):
                for s in PART[part.part]:
                    if s[0] in do:
                        do[s[0]](part, s, b + s[-1], *s[1:-1])

            n = units("lead")
            stages(Part("lead", 0), -1)
            stages(Part("first", n), 0)
            n += units("first")
            if at_part:
                at_part("body")
            with eng.Fori(1, B - 1) as b:
                stages(Part("body", n, (b - 1) * (units("body") // len(RING))), b)
            if at_part:
                at_part("final")
            n += (B - 2) * units("body")
            stages(Part("final", n), B - 1)
            stages(Part("tail", n + units("final")), B)

        @block.sync
        def _(sp):
            sp.dma_start(w1ld, W1.rearrange("(a p) n -> p a n", p=P)).then_inc(s_wffn, 16)
            sp.dma_start(w2ld, W2).then_inc(s_wffn, 16)
            sp.dma_start(b1c[:, :], b1.rearrange("(a p) -> p a", p=P),
                         allow_slow_non_contiguous=True).then_inc(s_wffn, 16)
            sp.dma_start(b2c[:, :], b2.rearrange("(p o) -> p o", o=1)).then_inc(s_wffn, 16)
            sp.dma_start(sc[:, :], row_of(scale).broadcast_to([P, 1])).then_inc(s_wffn, 16)
            sp.dma_start(om[:, :], row_of(omega).broadcast_to([P, H])).then_inc(s_wffn, 16)

            def load_weights(part, s, b):
                sp.dma_start(ub, row_of(u.rearrange("h d -> (h d)")).broadcast_to([P, HD])).then_inc(s_wload, 16)
                sp.dma_start(kwb[:, :], row_of(k_rms_w).broadcast_to([P, D])).then_inc(s_wload, 16)
                for i, w in enumerate((Wq, Wk, Wv)):
                    sp.dma_start(wld[:, i * HD:(i + 1) * HD], w).then_inc(s_wload, 16)
                sp.dma_start(wpl, Wproj.rearrange("(a p) n -> p a n", p=P)).then_inc(s_wload, 16)
                for n in range(2):
                    sp.dma_start(qw[n * D:(n + 1) * D, :], q_rms_w.rearrange("(p o) -> p o", o=1)).then_inc(s_unit, 16)
                    sp.dma_start(kw[n * D:(n + 1) * D, :], k_rms_w.rearrange("(p o) -> p o", o=1)).then_inc(s_unit, 16)
                sp.wait_ge(s_rows16, 1)
                sp.dma_start(q1[GROW:GROW + 4, :, :], rows16[0:4, :].unsqueeze(1).broadcast_to([4, H, T])).then_inc(s_rows, 16)
                sp.wait_ge(s_zeros, 1)
                sp.dma_start(k1[MROW:MROW + 1, :, :], rows16[4:5, :].unsqueeze(1).broadcast_to([1, H, T])).then_inc(s_rows, 16)

            def load_x(part, s, b, n):
                if n == "a":
                    if not (isinstance(b, int) and b == 0):
                        sp.wait_ge(s_var["att"], b)
                    sp.dma_start(x_in[:, :, :], x[b].rearrange("(t p) c -> p t c", p=P) if isinstance(b, int) else
                                 x[bass.ds(b, 1)].rearrange("o (t p) c -> p (o t) c", p=P)).then_inc(s_x, 16)

            def place_operands(part, s, b, hf):
                def place(dst, j, lo, done):
                    for n in range(2):
                        sp.dma_start(dst[:, hf * HH + n:(hf + 1) * HH:2, :],
                                     qkn16[n * D:(n + 1) * D, j, :, lo * T:(lo + 1) * T]).then_inc(done, 16)

                sp.wait_ge(s_hi, b * H + (hf + 1) * HH)
                place(q1[0:D, :, :], 0, 0, s_grow)
                place(k1[0:D, :, :], 1, 0, s_grow)
                part.taken(sp, ("gr", *s[1:]))
                for r in range(4):
                    sp.dma_start(k1[GROW + r:GROW + r + 1, hf * HH:(hf + 1) * HH, :],
                                 gtt[r * HH:(r + 1) * HH, :]).then_inc(s_grow, 16)
                place(q2[0:D, :, :], 0, 0, s_dup)
                place(k2[D:P, :, :], 1, 0, s_dup)
                part.taken(sp, ("t", 4 * hf + 3, s[-1]), 1)
                place(q2[D:P, :, :], 0, 1, s_dup)
                place(k2[0:D, :, :], 1, 1, s_dup)

            def max_rows(part, s, b, hf):
                part.taken(sp, s)
                sp.dma_start(q1[MROW:MROW + 1, hf * HH:(hf + 1) * HH, :], nmt[:, :]).then_inc(s_mrow, 16)

            def rows_and_parts(part, s, b, hf):
                gate_rows(part, ("gr", *s[1:]), b, hf)
                copy_parts(part, s, b, hf)

            def store(part, s, b, n):
                if n == "c":
                    part.taken(sp, s)
                    sp.dma_start(out[b].rearrange("(t p) c -> p t c", p=P) if isinstance(b, int) else
                                 out[bass.ds(b, 1)].rearrange("o (t p) c -> p (o t) c", p=P),
                                 x_out[:, :, :]).then_inc(s_out, 16)

            run(sp, {"weights": load_weights, "ln1": load_x, "rows": place_operands, "nm": max_rows, "back": store})
            sp.wait_ge(s_out, 16 * B)

        @block.gpsimd
        def _(pool):
            g = nc.gpsimd
            g.memset(ident[:, :], 0.0).then_inc(s_const, 1)
            g.memset(ident16[:, :], 0.0).then_inc(s_const, 1)
            g.memset(causal16[:, :], 0.0).then_inc(s_const, 1)
            g.memset(causal_t16[:, :], 0.0).then_inc(s_const, 1)
            g.memset(sel[:, :, :], 0.0).then_inc(s_const, 1)
            g.iota(jcol[:, :], [[P, TB]], base=-(T // 2), channel_multiplier=1,
                   allow_small_or_imprecise_dtypes=True).then_inc(s_const, 1)
            g.iota(icol, [[-1, T]], base=T // 2, channel_multiplier=0,
                   allow_small_or_imprecise_dtypes=True).then_inc(s_icol, 1)
            for t, n in ((rms_eps, RMS_EPS), (half, 0.5)):
                g.memset(t[:, :], n).then_inc(s_const, 1)
            for h, s in enumerate(slopes_of(H)):
                last = g.memset(slopes[:, h:h + 1], s)
            last.then_inc(s_const, 1)
            pool.wait_ge(s_const, 5)
            for m in (ident, ident16):
                g.affine_select(out=m[:, :], in_=m[:, :], compare_op=ALU.not_equal, fill=1.0, base=0,
                                pattern=[[-1, P]], channel_multiplier=1).then_inc(s_const, 1)
            g.affine_select(out=causal16[:, :], in_=causal16[:, :], compare_op=ALU.is_ge, fill=MASKED, base=0,
                            pattern=[[-1, P]], channel_multiplier=1).then_inc(s_const, 1)
            g.affine_select(out=causal_t16[:, :], in_=causal_t16[:, :], compare_op=ALU.is_ge, fill=MASKED, base=0,
                            pattern=[[1, P]], channel_multiplier=-1).then_inc(s_const, 1)
            for n, first in enumerate((2, 10, 1, 9)):
                s = sel[:, n, :].rearrange("p (r e) -> p r e", r=FB)
                g.affine_select(out=s, in_=s, compare_op=ALU.not_equal, fill=1.0, base=-first,
                                pattern=[[-2, FB], [1000, RPT]], channel_multiplier=1).then_inc(s_const, 1)
            pool.wait_ge(s_const, 17)
            g.memset(k1[D:P, :, :], 0.0).then_inc(s_zeros, 1)
            pool.wait_ge(s_zeros, 1)
            pool.wait_ge(s_setup, 1)

            def gate_weights(part, s, b):
                u3 = ub.rearrange("p (h n) -> p h n", h=H)
                uk3 = uk.rearrange("p (h n) -> p h n", h=H)
                k3 = wld[:, HD:2 * HD].rearrange("p (h n) -> p h n", h=H)
                pool.wait_ge(s_wload, 16 * 6)
                g.tensor_tensor(uk3, k3, u3, ALU.mult).then_inc(s_uk, 1)
                pool.wait_ge(s_uk, 1)
                g.tensor_tensor(uk3, uk3, kwb[:, :].unsqueeze(1).broadcast_to([P, H, D]), ALU.mult).then_inc(s_uk, 1)

            def length_of_u(part, s, b):
                pool.wait_ge(s_usq, 1)
                g.tensor_tensor(un[:, :], om_n[:, :], half[:, :], ALU.pow).then_inc(s_unorm, 1)

            def prepared(part, s, b):
                pool.wait_ge(s_prepared, 1)

            def exponentials_lo(part, s, b, h):
                n = b * H + h
                if not (isinstance(n, int) and n < 2):
                    pool.wait_ge(s_pv, n - 1)
                for j, (_, col, width) in enumerate(SBANK):
                    pool.wait_ge(s_exp, n * 3 + j + 1)
                    c = slice(col, col + width)
                    g.tensor_tensor(pt_l[:, h % 2, c], pt[:, h % 2, c], pt_h[:, h % 2, c], ALU.subtract).then_inc(s_pt_l, 1)

            def weights_lo(part, s, b, n):
                for i in range(2):
                    pool.wait_ge(s_w_h[n], b * 2 + i + 1)
                    g.tensor_tensor(w_l[:, i, :], weff[:, i, :], w_h[:, i, :], ALU.subtract).then_inc(s_w_l[n], 1)

            def hidden_lo(part, s, b, n):
                for r in range(FB):
                    pool.wait_ge(s_hid_h[n], b * FB + r + 1)
                    g.tensor_tensor(hid_l[:, r, :], hid[:, r % 2, :], hid_h[:, r, :], ALU.subtract).then_inc(s_hid_l[n], 1)

            def over_rms(part, s, b, hf, t):
                pool.wait_ge(s_rs, (b * 2 + hf) * TB + t + 1)
                for j in range(2):
                    qk = qkn[:, j, :, t * P:(t + 1) * P].rearrange("p i (h n) -> p i h n", n=D)
                    r = rs[:, t, j * HH:(j + 1) * HH].rearrange("p (i h) -> p i h", h=2)
                    g.tensor_tensor(qk, qk, r.unsqueeze(3).broadcast_to([P, HH // 2, 2, D]), ALU.mult).then_inc(s_qkn, 1)

            run(pool, {"weights": gate_weights, "prepare": length_of_u, "prepared": prepared, "pl": exponentials_lo,
                       "qkn": over_rms, "m": weights_lo, "h": hidden_lo})

        @block.scalar
        def _(act):
            a = nc.scalar
            act.preload_act_table_set(EXP_SET)
            act.wait_ge(s_omn, 1)
            a.activation(om_e[:, :], om_n[:, :], ACT.Exp).then_inc(s_oml, 1)
            act.wait_ge(s_oml, 1)
            a.activation(om_n[:, :], om_e[:, :], ACT.Ln, bias=1.0).then_inc(s_oml, 1)
            act.wait_ge(s_setup, 1)

            def attention_weights(part, s, b):
                act.wait_ge(s_wload, 16 * 6)
                a.activation(wqkv_h[:, :], wld, ACT.Copy, scale=QKV_UP).then_inc(s_whi, 1)
                a.activation(wp_h[:, :, :], wpl, ACT.Copy, scale=W_UP).then_inc(s_whi, 1)

            def prepared(part, s, b):
                act.wait_ge(s_prepared, 1)

            def zt_hi(part, s, b, n):
                for i in range(2):
                    part.full(act, s, i)
                    a.activation(zt_h[n][:, i * 2 * P:(i + 1) * 2 * P], part.bank(s, i)[:, 0:2 * P],
                                 ACT.Copy).then_inc(s_zt_h[n], 1)

            def gelu(part, s, b, n):
                for r in range(FB):
                    if r >= 2:
                        act.wait_ge(s_hid_l[n], b * FB + r - 1)
                    part.full(act, s, r)
                    part.taken_by(a.activation(hid[:, r % 2, :], part.bank(s, r), ACT.Gelu, bias=b1c[:, r:r + 1],
                                               scale=1.0 / W_UP), s, r)
                act.preload_act_table_set(EXP_SET)

            def ffn_out(part, s, b, n):
                part.full(act, s)
                part.taken_by(a.activation(o_ffn[:, :], part.bank(s), ACT.Identity, bias=b2half[:, :],
                                           scale=0.5 / W_UP), s)

            def take_qk(part, s, b, hf, t):
                g = b * 2 + hf
                if t == 0 and not (isinstance(g, int) and g == 0):
                    act.wait_ge(s_grow, g * 128)
                    act.wait_ge(s_dup, g * 128)
                blk = g * TB + t
                for j in range(2):
                    part.full(act, s, j)
                    if not (isinstance(blk, int) and blk < 2):
                        act.wait_ge(s_sqsum, (blk - 2) * 2 + j + 1)
                    a.activation(sq[:, t % 2, j, :], part.bank(s, j), ACT.Square).then_inc(s_sq, 1)
                    part.taken_by(a.activation(qkn[:, j, :, t * P:(t + 1) * P],
                                               part.bank(s, j).rearrange("p (i n) -> p i n", n=P), ACT.Copy), s, j)

            def inverse_rms(part, s, b, hf, t):
                blk = (b * 2 + hf) * TB + t
                act.wait_ge(s_sqsum, blk * 2 + 2)
                a.activation(ssl[:, t, :], ss[:, t, :], ACT.Ln, bias=rms_eps[:, :],
                             scale=1.0 / (D * QKV_UP * QKV_UP)).then_inc(s_ssl, 1)
                act.wait_ge(s_ssl, blk + 1)
                a.activation(rs[:, t, :], ssl[:, t, :], ACT.Exp, scale=-0.5).then_inc(s_rs, 1)

            def inverse_root(part, s, b, n):
                act.wait_ge(s_var[n], b + 1)
                a.activation(lnv[n][:, :], veps[n][:, :], ACT.Ln).then_inc(s_lnv[n], 1)
                act.wait_ge(s_lnv[n], b + 1)
                a.activation(rstd[n][:, :], lnv[n][:, :], ACT.Exp, scale=-0.5).then_inc(s_rstd[n], 1)

            def gate_softplus(part, s, b, hf):
                act.wait_ge(s_lga, b * 2 + hf + 1)
                a.activation(lge[:, :, :], lga[:, :, :], ACT.Exp).then_inc(s_lge, 1)
                act.wait_ge(s_lge, b * 2 + hf + 1)
                a.activation(lgl[:, :, :], lge[:, :, :], ACT.Ln, bias=1.0).then_inc(s_lgl, 1)

            def hi_parts(part, s, b, p):
                for j, w in enumerate((qws, kws)):
                    part.full(act, s, j)
                    a.activation(qkn16[:, j, p % 4, 0:T], part.bank(s, j), ACT.Identity, scale=w[:, :]).then_inc(s_hi, 1)

            def v_hi(part, s, b, j, t):
                part.full(act, s)
                a.activation(v_hl[:, 0, t, j * HH:(j + 1) * HH, 0:D], part.bank(s).rearrange("p (h n) -> p h n", n=D),
                             ACT.Copy).then_inc(s_v_h, 1)

            def exponentials(part, s, b, h):
                n = b * H + h
                if not (isinstance(n, int) and n < 2):
                    act.wait_ge(s_pv, n - 1)
                for j, (_, col, width) in enumerate(SBANK):
                    if not (isinstance(n, int) and n < 2):
                        act.wait_ge(s_pt_l, (n - 2) * 3 + j + 1)
                    act.wait_ge(s_s_ps, n * 3 + j + 1)
                    c = slice(col, col + width)
                    a.activation(pt[:, h % 2, c], ps[:, j, 0:width], ACT.Exp)
                    a.activation(pt_h[:, h % 2, c], ps[:, j, 0:width], ACT.Exp).then_inc(s_exp, 1)

            def y_hi(part, s, b, p):
                part.full(act, s)
                a.activation(y_h[:, p % 2, :], part.bank(s), ACT.Copy).then_inc(s_y_h, 1)

            run(act, {"weights": attention_weights, "prepared": prepared, "ln1": inverse_root, "qkn": inverse_rms, "zt":
                      zt_hi, "h": gelu, "out": ffn_out, "qk": take_qk, "gate": gate_softplus, "t": hi_parts,
                      "v": v_hi, "s": exponentials, "yt": y_hi})

        @block.tensor
        def _(pe):
            pe.wait_ge(s_const, 17)
            pe.wait_ge(s_wffn, 16 * 6)
            for r in range(FB):
                pe.transpose(ps[:, 0, r * P:(r + 1) * P], w1ld[:, r, :], ident[:, :]).then_inc(s_w12_ps, 1)
            for r in range(FB):
                pe.transpose(ps[:, 1, r * P:(r + 1) * P], w2ld[:, r * P:(r + 1) * P], ident[:, :]).then_inc(s_w12_ps, 1)
            pe.wait_ge(s_setup, 1)

            def prepared(part, s, b):
                pe.wait_ge(s_prepared, 1)
                pe.wait_ge(s_rows, 32)

            def product(dst, ah, al, bh, bl, first=True, last=True):
                pe.matmul(dst, ah, bh, start=first, stop=False)
                pe.matmul(dst, ah, bl, start=False, stop=False)
                return pe.matmul(dst, al, bh, start=False, stop=last)

            def turn(part, s, src):
                part.room(pe, s)
                for t in range(TB):
                    mm = pe.transpose(part.bank(s)[:, t * P:(t + 1) * P], src(t), ident[:, :])
                part.filled_by(mm, s)

            def zt(part, s, b, n):
                for i in range(2):
                    pe.wait_ge(s_z[n], b * TB + 2 * i + 2)
                    part.room(pe, s, i)
                    for t in range(2):
                        mm = pe.transpose(part.bank(s, i)[:, t * P:(t + 1) * P], z[n][:, 2 * i + t, :], ident[:, :])
                    part.filled_by(mm, s, i)

            def adapter_vectors(part, s, b, n):
                pe.wait_ge(s_z[n], b * TB + 1)
                for i in range(2):
                    part.room(pe, s, i)
                    for f in range(2):
                        mm = pe.matmul(part.bank(s, i)[:, f * P:(f + 1) * P], sel[:, 2 * i + f, :], z[n][:, 0, :],
                                       start=True, stop=True)
                    part.filled_by(mm, s, i)

            def adapter_blocks(part, s, b, n):
                for i in range(2):
                    part.taken(pe, ("sel", *s[1:]), i, then=s)
                for i in range(2):
                    part.room(pe, s, i)
                    part.filled_by(pe.matmul(part.bank(s, i), od[:, i, :], ev[:, i, :], start=True, stop=True), s, i)

            def hidden(part, s, b, n):
                pe.wait_ge(s_w_l[n], (b + 1) * 2)
                part.taken(pe, ("zt", *s[1:]), 1, then=s)
                for r in range(FB):
                    c = slice(r * P, (r + 1) * P)
                    part.room(pe, s, r)
                    part.filled_by(product(part.bank(s, r), w_h[:, 0, c], w_l[:, 0, c], zt_h[n][:, :], zt_l[n][:, :]), s, r)

            def ffn_out(part, s, b, n):
                part.room(pe, s)
                for r in range(FB):
                    pe.wait_ge(s_hid_l[n], b * FB + r + 1)
                    c = slice(r * P, (r + 1) * P)
                    mm = product(part.bank(s), w_h[:, 1, c], w_l[:, 1, c], hid_h[:, r, :], hid_l[:, r, :], r == 0, r == FB - 1)
                part.filled_by(mm, s)

            def ffn_back(part, s, b, n):
                part.taken(pe, ("out", *s[1:]), then=s)
                turn(part, s, lambda t: o_ffn[:, t * P:(t + 1) * P])

            def project_qk(part, s, b, hf, t):
                if (hf, t) == (0, 0):
                    part.taken(pe, ("zt", "att", s[-1]), 1, then=s)
                for j in range(2):
                    w = slice(j * HD + hf * 512, j * HD + hf * 512 + 512)
                    c = slice(t * P, (t + 1) * P)
                    part.room(pe, s, j)
                    part.filled_by(product(part.bank(s, j), zt_h["att"][:, c], zt_l["att"][:, c], wqkv_h[:, w],
                                           wqkv_l[:, w]), s, j)

            def project_v(part, s, b, j, t):
                w = slice(2 * HD + j * 512, 2 * HD + j * 512 + 512)
                c = slice(t * P, (t + 1) * P)
                part.room(pe, s)
                part.filled_by(product(part.bank(s), zt_h["att"][:, c], zt_l["att"][:, c], wqkv_h[:, w], wqkv_l[:, w]), s)

            def gate_logits(part, s, b, hf):
                w = slice(hf * HH, (hf + 1) * HH)
                part.room(pe, s)
                for t in range(TB):
                    c = slice(t * P, (t + 1) * P)
                    mm = product(part.bank(s)[:, t * HH:(t + 1) * HH], zt_h["att"][:, c], zt_l["att"][:, c], wu_h[:, w],
                                 wu_l[:, w])
                part.filled_by(mm, s)

            def gate_rows(part, s, b, hf):
                pe.wait_ge(s_gt, b * 2 + hf + 1)
                part.room(pe, s)
                for t in range(TB):
                    mm = pe.transpose(part.bank(s)[0:4 * HH, :].bitcast(F16)[:, t * P:(t + 1) * P],
                                      gt[:, t, :, :].rearrange("p r h -> p (r h)"), ident16[:, :])
                part.filled_by(mm, s)

            def turn_heads(part, s, b, p):
                pe.wait_ge(s_qkn, (b * 2 + p // 4 + 1) * TB * 2)
                for j in range(2):
                    part.room(pe, s, j)
                    for t in range(TB):
                        mm = pe.transpose(part.bank(s, j)[:, t * P:(t + 1) * P],
                                          qkn[:, j, p % 4, t * P:(t + 1) * P], ident[:, :])
                    part.filled_by(mm, s, j)

            def max_scores(part, s, b, h):
                pe.wait_ge(s_grow, (b * 2 + h // HH + 1) * 128)
                for i, blocks in enumerate(((3,), (2, 0), (1,))):
                    part.room(pe, s, i)
                    for ib in blocks:
                        keys = (ib + 1) * P
                        col = 384 if len(blocks) == 2 and ib == 0 else 0
                        dst = part.bank(s, i)[:, col:col + keys]
                        pe.matmul(dst, q1[0:MROW, h, ib * P:keys], k1[0:MROW, h, 0:keys], start=True, stop=False)
                        mm = pe.matmul(dst[:, ib * P:keys], ident16[:, :], causal16[:, :], start=False, stop=True)
                    part.filled_by(mm, s, i)

            def turn_max(part, s, b, hf):
                part.taken(pe, ("a", hf * HH + HH - 1, s[-1]), 2, then=s)
                part.room(pe, s)
                for t in range(TB):
                    mm = pe.transpose(part.bank(s)[0:HH, :].bitcast(F16)[:, t * P:(t + 1) * P],
                                      negm[:, t, hf * HH:(hf + 1) * HH], ident16[:, :])
                part.filled_by(mm, s)

            def scores(part, s, b, h):
                n = b * H + h
                if h % HH == 0:
                    pe.wait_ge(s_mrow, (b * 2 + h // HH + 1) * 16)
                    pe.wait_ge(s_dup, (b * 2 + h // HH + 1) * 128)
                for j, (blocks, first, _) in enumerate(SBANK):
                    if not (isinstance(n, int) and n == 0):
                        pe.wait_ge(s_exp, (n - 1) * 3 + j + 1)
                    for kb in blocks:
                        col, width = REGION[kb]
                        dst = ps[:, j, col - first:col - first + width]
                        keys = slice(kb * P, kb * P + P)
                        pe.matmul(dst, k1[:, h, keys], q1[:, h, kb * P:T], start=True, stop=False)
                        pe.matmul(dst, k2[:, h, keys], q2[:, h, kb * P:T], start=False, stop=False)
                        mm = pe.matmul(dst[:, 0:P], ident16[:, :], causal_t16[:, :], start=False, stop=True)
                    mm.then_inc(s_s_ps, 1)

            def weighted(part, s, b, h):
                n = b * H + h
                pe.wait_ge(s_exp, (n + 1) * 3)
                pe.wait_ge(s_pt_l, (n + 1) * 3)
                if isinstance(n, int) and n == 0:
                    for t in range(TB):
                        Part("lead", 0).taken(pe, ("v", 0, t, NEXT))
                else:
                    pe.wait_ge(s_y, n)
                for ib in range(TB):
                    dst = ps[:, Y_BANK, ib * (D + 1):(ib + 1) * (D + 1)]
                    for kb in range(ib + 1):
                        col = REGION[kb][0] + (ib - kb) * P
                        c = slice(col, col + P)
                        mm = product(dst, pt_h[:, h % 2, c], pt_l[:, h % 2, c], v_hl[:, 0, kb, h, :], v_hl[:, 1, kb, h, :],
                                     kb == 0, kb == ib)
                mm.then_inc(s_pv, 1)

            def turn_y(part, s, b, p):
                pe.wait_ge(s_y, b * H + 2 * p + 2)
                turn(part, s, lambda t: ytok[:, p % 2, t, :])

            def project_out(part, s, b, i):
                part.taken(pe, ("yt", 2 * i + 1, s[-1]), then=s)
                part.room(pe, s)
                for t in range(TB):
                    c = slice(t * P, (t + 1) * P)
                    for n in range(2):
                        mm = product(part.bank(s)[:, c], y_h[:, n, c], y_l[:, n, c], wp_h[:, 2 * i + n, :],
                                     wp_l[:, 2 * i + n, :], n == 0, n == 1)
                part.filled_by(mm, s)

            run(pe, {"prepared": prepared, "zt": zt, "sel": adapter_vectors, "m": adapter_blocks, "h": hidden, "out":
                     ffn_out, "back": ffn_back,
                     "qk": project_qk, "v": project_v, "gl": gate_logits, "gr": gate_rows,
                     "t": turn_heads, "a": max_scores, "nm": turn_max, "s": scores, "pv": weighted, "yt": turn_y,
                     "wp": project_out})

        @block.vector
        def _(dve):
            d = nc.vector
            steps = {"n": 0, "start": None}
            PER_ITERATION = 16

            def link(ins, rounds=0):
                steps["n"] += 1
                ins.then_inc(dve_step, 1)
                dve.wait_ge(dve_step, rounds * PER_ITERATION + steps["n"])

            def at_part(part):
                if part == "body":
                    steps["start"] = steps["n"]
                else:
                    assert steps["n"] - steps["start"] == PER_ITERATION, steps
                    steps["n"] = steps["start"] + (B - 2) * PER_ITERATION

            link(d.memset(rows16[0:5, :], 1.0))
            dve.wait_ge(s_icol, 1)
            d.tensor_copy(rows16[0:2, :], icol[0:2, :])
            d.memset(ev[:, :, :], 0.0)
            d.memset(q1[D:P, :, :], 0.0).then_inc(s_rows16, 1)
            dve.wait_ge(s_wffn, 16 * 6)
            d.tensor_scalar(b2half[:, :], b2c[:, :], 0.5, None, ALU.mult)
            d.tensor_scalar(sc_up[:, :], sc[:, :], W_UP, None, ALU.mult)
            link(d.tensor_scalar(om_e[:, :], om[:, :], -1.0, None, ALU.mult))
            d.tensor_tensor(om_n[:, :], om[:, :], om_e[:, :], ALU.min).then_inc(s_omn, 1)
            dve.wait_ge(s_w12_ps, 2 * FB)
            d.tensor_scalar(w1s[:, :], ps[:, 0, :], W_UP, None, ALU.mult)
            d.tensor_scalar(w2s[:, :], ps[:, 1, :], W_UP, None, ALU.mult).then_inc(s_setup, 1)
            dve.wait_ge(s_setup, 1)

            def attention_weights(part, s, b):
                dve.wait_ge(s_oml, 2)
                link(d.scalar_tensor_tensor(om[:, :], om[:, :], 0.0, om_n[:, :], ALU.max, ALU.add))
                dve.wait_ge(s_const, 17)
                link(d.tensor_tensor(om[:, :], om[:, :], slopes[:, :], ALU.mult))
                dve.wait_ge(s_wload, 16 * 6)
                dve.wait_ge(s_unit, 64)
                link(d.tensor_tensor(usq, ub, ub, ALU.mult))
                d.tensor_reduce(om_n[:, :], usq.rearrange("p (h n) -> p h n", h=H), AX.X, ALU.add).then_inc(s_usq, 1)
                dve.wait_ge(s_whi, 1)
                d.scalar_tensor_tensor(wqkv_l[:, :], wld, QKV_UP, wqkv_h[:, :], ALU.mult, ALU.subtract)
                dve.wait_ge(s_whi, 2)
                d.scalar_tensor_tensor(wp_l[:, :, :], wpl, W_UP, wp_h[:, :, :], ALU.mult, ALU.subtract)
                d.tensor_scalar(qws[:, :], qw[:, :], 1.0 / (math.sqrt(D) * QKV_UP), None, ALU.mult)
                d.tensor_scalar(kws[:, :], kw[:, :], 1.0 / QKV_UP, None, ALU.mult)
                dve.wait_ge(s_uk, 2)
                d.tensor_reduce(wu[:, :], uk.rearrange("p (h n) -> p h n", h=H), AX.X, ALU.add)
                dve.wait_ge(s_unorm, 1)
                link(d.tensor_scalar(un[:, :], un[:, :], U_EPS, None, ALU.max))
                link(d.reciprocal(un[:, :], un[:, :]))
                link(d.scalar_tensor_tensor(wu[:, :], wu[:, :], W_UP / math.sqrt(D), un[:, :], ALU.mult, ALU.mult))
                link(d.tensor_copy(wu_h[:, :], wu[:, :]))
                d.tensor_tensor(wu_l[:, :], wu[:, :], wu_h[:, :], ALU.subtract)
                d.memset(v_hl[:, 0, :, :, D:D + 1], 1.0)
                d.memset(v_hl[:, 1, :, :, D:D + 1], 0.0).then_inc(s_prepared, 1)
                dve.wait_ge(s_prepared, 1)

            def statistics(part, s, b, n):
                src = {"a": x_in, "att": x_1, "c": x_2}[n]
                if n == "a":
                    dve.wait_ge(s_x, (b + 1) * 16)
                r = rounds(b, s)
                for t in range(TB):
                    ins = d.bn_stats(stats[n][:, t, :], src[:, t, :])
                link(ins, r)
                d.memset(veps[n][:, :], LN_EPS)
                for t in range(TB):
                    ins = d.bn_aggr(mv[n][:, t, :], stats[n][:, t, :])
                link(ins, r)
                d.tensor_tensor(veps[n][:, :], mv[n][:, :, 1], veps[n][:, :], ALU.add).then_inc(s_var[n], 1)

            def rounds(b, s):
                return 0 if isinstance(b, int) else b - s[-1] - 1

            def normalize(part, s, b, n):
                src = {"a": x_in, "att": x_1, "c": x_2}[n]
                dve.wait_ge(s_rstd[n], b + 1)
                for t in range(TB):
                    d.tensor_scalar(z[n][:, t, :], src[:, t, :], mv[n][:, t, 0:1], rstd[n][:, t:t + 1], ALU.subtract,
                                    ALU.mult).then_inc(s_z[n], 1)

            def zt_lo(part, s, b, n):
                for i in range(2):
                    c = slice(i * 2 * P, (i + 1) * 2 * P)
                    part.full(dve, s, i)
                    dve.wait_ge(s_zt_h[n], b * 2 + i + 1)
                    part.taken_by(d.tensor_tensor(zt_l[n][:, c], part.bank(s, i)[:, 0:2 * P], zt_h[n][:, c], ALU.subtract), s, i)

            def adapter_factors(part, s, b, n):
                part.full(dve, s, 0)
                part.taken_by(d.tensor_copy(od[:, :, :].rearrange("p a n -> p (a n)"), part.bank(s, 0)[:, 0:2 * P]), s, 0)
                part.full(dve, s, 1)
                for r in range(FB):
                    rows = slice(r * RPT, (r + 1) * RPT)
                    d.tensor_copy(ev[rows, 0, r * P:(r + 1) * P], part.bank(s, 1)[rows, 0:P])
                    dst = ev[rows, 1, :].rearrange("p (k r q) -> p k r q", k=FB, r=FB)[:, :, r, :]
                    ins = d.tensor_copy(dst, part.bank(s, 1)[rows, P:2 * P].rearrange("p (q k) -> p k q", k=FB))
                part.taken_by(ins, s, 1)

            def adapted_weights(part, s, b, n):
                for i, w in enumerate((w1s, w2s)):
                    part.full(dve, s, i)
                    part.taken_by(d.scalar_tensor_tensor(weff[:, i, :], part.bank(s, i), sc_up[:, :], w[:, :], ALU.mult,
                                                         ALU.add), s, i)
                    part.taken(dve, s, i)
                    d.tensor_copy(w_h[:, i, :], weff[:, i, :]).then_inc(s_w_h[n], 1)

            def hidden_hi(part, s, b, n):
                for r in range(FB):
                    part.taken(dve, s, r)
                    d.tensor_copy(hid_h[:, r, :], hid[:, r % 2, :]).then_inc(s_hid_h[n], 1)

            def add_ffn(part, s, b, n):
                src, dst = {"a": (x_in, x_1), "c": (x_2, x_out)}[n]
                if n == "c" and not (isinstance(b, int) and b == 0):
                    dve.wait_ge(s_out, 16 * b)
                add(part, s, src, dst)

            def add(part, s, src, dst):
                part.full(dve, s)
                part.taken_by(d.tensor_tensor(dst[:, :, :].rearrange("p t c -> p (t c)"), part.bank(s),
                                              src[:, :, :].rearrange("p t c -> p (t c)"), ALU.add), s)
                part.taken(dve, s)

            def add_attention(part, s, b, i):
                src, dst = x_1 if i == 0 else x_att, x_2 if i == NP // 2 - 1 else x_att
                part.full(dve, s)
                part.taken_by(d.scalar_tensor_tensor(dst[:, :, :].rearrange("p t c -> p (t c)"), part.bank(s),
                                                     1.0 / (W_UP * QKV_UP), src[:, :, :].rearrange("p t c -> p (t c)"),
                                                     ALU.mult, ALU.add), s)
                part.taken(dve, s)

            def square_sums(part, s, b, hf, t):
                blk = (b * 2 + hf) * TB + t
                for j in range(2):
                    dve.wait_ge(s_sq, blk * 2 + j + 1)
                    d.tensor_reduce(ss[:, t, j * HH:(j + 1) * HH], sq[:, t % 2, j, :].rearrange("p (h n) -> p h n", n=D), AX.X,
                                    ALU.add).then_inc(s_sqsum, 1)

            def take_logits(part, s, b, hf):
                r = rounds(b, s)
                part.full(dve, s)
                dve.wait_ge(s_rs, (b * 2 + hf + 1) * TB)
                part.taken_by(d.scalar_tensor_tensor(lg[:, :, :], part.bank(s)[:, 0:TB * HH].rearrange("p (t h) -> p t h", h=HH),
                                                     1.0 / W_UP, rs[:, :, HH:2 * HH], ALU.mult, ALU.mult), s)
                part.taken(dve, s)
                link(d.tensor_scalar(lgn[:, :, :], lg[:, :, :], -1.0, None, ALU.mult), r)
                d.tensor_tensor(lga[:, :, :], lg[:, :, :], lgn[:, :, :], ALU.min).then_inc(s_lga, 1)

            def gates(part, s, b, hf):
                r = rounds(b, s)
                dve.wait_ge(s_lgl, b * 2 + hf + 1)
                link(d.scalar_tensor_tensor(softplus[:, :, :], lg[:, :, :], 0.0, lgl[:, :, :], ALU.max, ALU.add), r)
                link(d.tensor_tensor(gate[:, :, :], softplus[:, :, :],
                                     om[:, hf * HH:(hf + 1) * HH].unsqueeze(1).broadcast_to([P, TB, HH]), ALU.mult), r)
                link(d.tensor_tensor(jgate[:, :, :], gate[:, :, :], jcol[:, :].unsqueeze(2).broadcast_to([P, TB, HH]),
                                     ALU.mult), r)
                d.tensor_copy(gt[:, :, 0, :], gate[:, :, :])
                link(d.tensor_copy(gt[:, :, 2, :], jgate[:, :, :]), r)
                d.tensor_tensor(gt[:, :, 1, :], gate[:, :, :], gt[:, :, 0, :], ALU.subtract)
                d.tensor_tensor(gt[:, :, 3, :], jgate[:, :, :], gt[:, :, 2, :], ALU.subtract).then_inc(s_gt, 1)

            def take_gate_rows(part, s, b, hf):
                part.full(dve, s)
                g = b * 2 + hf
                if not (isinstance(g, int) and g == 0):
                    dve.wait_ge(s_grow, g * 128)
                part.taken_by(d.tensor_copy(gtt[:, :], part.bank(s)[0:4 * HH, :].bitcast(F16)[:, 0:T]), s)

            def lo_parts(part, s, b, p):
                for j, w in enumerate((qws, kws)):
                    part.full(dve, s, j)
                    dve.wait_ge(s_hi, b * H + p * 2 + j + 1)
                    part.taken_by(d.scalar_tensor_tensor(qkn16[:, j, p % 4, T:2 * T], part.bank(s, j), w[:, :],
                                                         qkn16[:, j, p % 4, 0:T], ALU.mult, ALU.subtract), s, j)

            def maxima(part, s, b, h):
                for i, blocks in enumerate(((3,), (2, 0), (1,))):
                    part.full(dve, s, i)
                    for ib in blocks:
                        col = 384 if len(blocks) == 2 and ib == 0 else 0
                        ins = d.tensor_reduce(negm[:, ib, h:h + 1], part.bank(s, i)[:, col:col + (ib + 1) * P], AX.X, ALU.max,
                                              negate=True)
                    part.taken_by(ins, s, i)

            def take_max_rows(part, s, b, hf):
                part.full(dve, s)
                g = b * 2 + hf
                if not (isinstance(g, int) and g == 0):
                    dve.wait_ge(s_mrow, g * 16)
                part.taken_by(d.tensor_copy(nmt[:, :], part.bank(s)[0:HH, :].bitcast(F16)[:, 0:T]), s)

            def over_sums(part, s, b, h):
                n = b * H + h
                y = ps[:, Y_BANK, 0:TB * (D + 1)].rearrange("p (t n) -> p t n", n=D + 1)
                dve.wait_ge(s_pv, n + 1)
                d.reciprocal(rden[:, :], y[:, :, D]).then_inc(s_rden, 1)
                dve.wait_ge(s_rden, n + 1)
                d.tensor_tensor(ytok[:, (h // 2) % 2, :, (h % 2) * D:(h % 2 + 1) * D], y[:, :, 0:D],
                                rden[:, :].unsqueeze(2).broadcast_to([P, TB, D]), ALU.mult).then_inc(s_y, 1)

            def v_lo(part, s, b, j, t):
                part.full(dve, s)
                dve.wait_ge(s_v_h, (b * 2 + j) * TB + t + 1)
                hs = slice(j * HH, (j + 1) * HH)
                part.taken_by(d.tensor_tensor(v_hl[:, 1, t, hs, 0:D], part.bank(s).rearrange("p (h n) -> p h n", n=D),
                                              v_hl[:, 0, t, hs, 0:D], ALU.subtract), s)

            def y_lo(part, s, b, p):
                part.full(dve, s)
                dve.wait_ge(s_y_h, b * NP + p + 1)
                part.taken_by(d.tensor_tensor(y_l[:, p % 2, :], part.bank(s), y_h[:, p % 2, :], ALU.subtract), s)

            run(dve, {"prepare": attention_weights, "ln1": statistics, "ln2": normalize, "zt": zt_lo, "sel":
                      adapter_factors, "m": adapted_weights, "h": hidden_hi,
                      "back": add_ffn, "wp": add_attention, "qk": square_sums,
                      "gl": take_logits, "gate": gates, "gr": take_gate_rows, "t": lo_parts, "a": maxima,
                      "nm": take_max_rows, "pv": over_sums, "v": v_lo, "yt": y_lo}, at_part)


_INS = ["L0_attn_x", "L0_attn_Wq", "L0_attn_Wk", "L0_attn_Wv", "L0_attn_Wproj", "L0_attn_q_rms_w", "L0_attn_k_rms_w",
        "L0_attn_omega", "L0_attn_u", "L0_ffn_W1", "L0_ffn_b1", "L0_ffn_W2", "L0_ffn_b2", "L0_ffn_scale"]


def kernel(**inputs):
    import numpy as np
    import concourse.bacc as bacc
    from concourse.bass_utils import run_bass_kernel_spmd

    nc = bacc.Bacc("TRN2", target_bir_lowering=False, num_devices=1)
    arrays, args = {}, []
    for name in _INS:
        a = np.ascontiguousarray(inputs[name])
        a = a.reshape(a.shape or (1,))
        arrays[f"in_{name}"] = a
        args.append(nc.dram_tensor(f"in_{name}", a.shape, mybir.dt.from_np(a.dtype), kind="ExternalInput").ap())
    shape = arrays["in_L0_attn_x"].shape
    args.append(nc.dram_tensor("out_0", shape, F32, kind="ExternalOutput").ap())
    macaron(nc, *args)
    r = run_bass_kernel_spmd(nc, [arrays], core_ids=[0])
    return r.results[0]["out_0"]
```
